# Optimizing a Trainium2 kernel written in Bass

```python
import numpy as np
import jax
import jax.numpy as jnp

def _softmax(x, axis=-1):
    return jax.nn.softmax(x, axis=axis)

def _gelu(x):
    return jax.nn.gelu(x, approximate=True)

def _silu(x):
    return jax.nn.silu(x)

def _sigmoid(x):
    return jax.nn.sigmoid(x)

def _layernorm(x, axis=-1, eps=1e-05):
    m = jnp.mean(x, axis=axis, keepdims=True)
    v = jnp.var(x, axis=axis, keepdims=True)
    return (x - m) / jnp.sqrt(v + eps)

def _scatter_add(tgt, idx, src, axis=0):
    return tgt.at[idx].add(src)

def _segment_sum(src, seg, n):
    return jax.ops.segment_sum(src, seg, n)
kernel_name = 'mk_pixart_resid_d1_seqx_r8_bc4d80'

def setup_inputs(seed: int=0):
    np.random.seed(seed)
    _w = jnp.asarray

    def _rec_inputs():
        import jax
        import jax.numpy as jnp
        _rk = jax.random.key(seed)
        x = 7.22e-05 + 1 * jax.random.normal(jax.random.fold_in(_rk, 1), (16, 128, 128), jnp.float32)
        _lenS = 128 - jax.random.randint(jax.random.fold_in(_rk, 7), (16,), 0, max(1, 128 // 4) + 1, jnp.int32)
        _lenS2 = 128 - jax.random.randint(jax.random.fold_in(_rk, 8), (16,), 0, max(1, 128 // 4) + 1, jnp.int32)
        _ctx_1024P = jax.random.normal(jax.random.fold_in(_rk, 11), (16, 16, 128), jnp.float32)
        _ctx_1024c = jax.random.dirichlet(jax.random.fold_in(_rk, 511), 0.3 * jnp.ones((16,), jnp.float32), (16, 128))
        _ctx_1024t = jnp.einsum('bsk,bkd->bsd', _ctx_1024c, _ctx_1024P)
        _ctx_1024t = _ctx_1024t * jax.lax.rsqrt(jnp.mean(jnp.square(_ctx_1024t)) + 1e-12) * 0.953939
        ctx_1024 = 5.54337e-07 + 0.0180436 * (_ctx_1024t + 0.3 * jax.random.normal(jax.random.fold_in(_rk, 611), (16, 128, 128), jnp.float32))
        cond_1024 = 0.000192168 + 0.0182672 * jax.random.normal(jax.random.fold_in(_rk, 12), (16, 128), jnp.float32)
        return (x, ctx_1024, cond_1024)
    x, ctx_1024, cond_1024 = _rec_inputs()

    def _L0_xcond_setup():
        import jax, jax.numpy as jnp
        import numpy as np
        B, S, H, L = (4, 256, 128, 4)
        CLAMP_LO, CLAMP_HI = (1e-08, 1.0 - 1e-08)
        LN_EPS = 1e-05

        def _linear_scan(a, b):

            def combine(left, right):
                al, bl = left
                ar, br = right
                return (ar * al, ar * bl + br)
            _, h = jax.lax.associative_scan(combine, (a, b), axis=1)
            return h

        def _mingru(x, Wz, bz, Wh, bh):
            z = jax.nn.sigmoid(jnp.einsum('bsi,hi->bsh', x, Wz) + bz)
            h_tilde = jnp.tanh(jnp.einsum('bsi,hi->bsh', x, Wh) + bh)
            a = jnp.clip(1.0 - z, CLAMP_LO, CLAMP_HI)
            return _linear_scan(a, z * h_tilde)

        def _layernorm(x, gamma, beta):
            mu = jnp.mean(x, axis=-1, keepdims=True)
            var = jnp.mean(jnp.square(x - mu), axis=-1, keepdims=True)
            return (x - mu) * jax.lax.rsqrt(var + LN_EPS) * gamma + beta

        def _stack(x, Wz, bz, Wh, bh, gamma, beta):
            h = x
            for i in range(L):
                h_new = _mingru(h, Wz[i], bz[i], Wh[i], bh[i])
                if i > 0:
                    h_new = h_new + h
                h = _layernorm(h_new, gamma, beta)
            return h
        key = jax.random.key(seed)
        ks = jax.random.split(key, 13)
        s = 1.0 / np.sqrt(H)
        u = lambda k, shape: jax.random.uniform(k, shape, jnp.float32, -s, s)
        return {'x': jax.random.normal(ks[0], (B, S, H), jnp.float32), 'fwd_Wz': u(ks[1], (L, H, H)), 'fwd_bz': u(ks[2], (L, H)), 'fwd_Wh': u(ks[3], (L, H, H)), 'fwd_bh': u(ks[4], (L, H)), 'bwd_Wz': u(ks[5], (L, H, H)), 'bwd_bz': u(ks[6], (L, H)), 'bwd_Wh': u(ks[7], (L, H, H)), 'bwd_bh': u(ks[8], (L, H)), 'fusion_W': u(ks[9], (H, 2 * H)), 'fusion_b': u(ks[10], (H,)), 'ln_gamma': jnp.ones((H,), jnp.float32), 'ln_beta': jnp.zeros((H,), jnp.float32)}
    _L0_xcond_all = _L0_xcond_setup()
    _L0_xcond_in = {k: v for k, v in _L0_xcond_all.items() if k in ('fusion_W', 'fusion_b', 'ln_gamma', 'ln_beta')}
    del _L0_xcond_all

    def _L0_ffn_setup():
        import jax, jax.numpy as jnp
        import numpy as np
        D_MODEL = 128
        N_HEAD = 16
        HEAD_DIM = D_MODEL // N_HEAD
        D_FF = 512
        N_EXPERTS = 4
        EPS = 1e-05

        def _layer_norm(x, gamma, beta):
            mu = jnp.mean(x, axis=-1, keepdims=True)
            var = jnp.mean((x - mu) ** 2, axis=-1, keepdims=True)
            return (x - mu) / jnp.sqrt(var + EPS) * gamma + beta
        key = jax.random.key(seed)
        ks = jax.random.split(key, 20)
        f32 = jnp.float32
        sc = 1.0 / np.sqrt(D_MODEL)
        scf = 1.0 / np.sqrt(D_FF)
        return {'src': jax.random.normal(ks[0], (4, 64, D_MODEL), f32), 'Wq': jax.random.normal(ks[1], (D_MODEL, D_MODEL), f32) * sc, 'bq': jnp.zeros((D_MODEL,), f32), 'Wk': jax.random.normal(ks[2], (D_MODEL, D_MODEL), f32) * sc, 'bk': jnp.zeros((D_MODEL,), f32), 'Wv': jax.random.normal(ks[3], (D_MODEL, D_MODEL), f32) * sc, 'bv': jnp.zeros((D_MODEL,), f32), 'Wo': jax.random.normal(ks[4], (D_MODEL, D_MODEL), f32) * sc, 'bo': jnp.zeros((D_MODEL,), f32), 'router_w': jax.random.normal(ks[5], (D_MODEL, 1), f32) * 0.05, 'router_b': jnp.zeros((1,), f32), 'W1': jax.random.normal(ks[6], (N_EXPERTS, D_MODEL, D_FF), f32) * sc, 'b1': jnp.zeros((N_EXPERTS, D_FF), f32), 'W2': jax.random.normal(ks[7], (N_EXPERTS, D_FF, D_MODEL), f32) * scf, 'b2': jnp.zeros((N_EXPERTS, D_MODEL), f32), 'ln1_g': jnp.ones((D_MODEL,), f32), 'ln1_b': jnp.zeros((D_MODEL,), f32), 'ln2_g': jnp.ones((D_MODEL,), f32), 'ln2_b': jnp.zeros((D_MODEL,), f32)}
    _L0_ffn_all = _L0_ffn_setup()
    _L0_ffn_in = {k: v for k, v in _L0_ffn_all.items() if k in ('Wq', 'bq', 'Wk', 'bk', 'Wv', 'bv', 'Wo', 'bo', 'router_w', 'router_b', 'W1', 'b1', 'W2', 'b2', 'ln1_g', 'ln1_b', 'ln2_g', 'ln2_b')}
    del _L0_ffn_all
    return {'x': x, 'ctx_1024': ctx_1024, 'cond_1024': cond_1024, 'L0_xcond_fusion_W': _L0_xcond_in['fusion_W'], 'L0_xcond_fusion_b': _L0_xcond_in['fusion_b'], 'L0_xcond_ln_gamma': _L0_xcond_in['ln_gamma'], 'L0_xcond_ln_beta': _L0_xcond_in['ln_beta'], 'L0_ffn_Wq': _L0_ffn_in['Wq'], 'L0_ffn_bq': _L0_ffn_in['bq'], 'L0_ffn_Wk': _L0_ffn_in['Wk'], 'L0_ffn_bk': _L0_ffn_in['bk'], 'L0_ffn_Wv': _L0_ffn_in['Wv'], 'L0_ffn_bv': _L0_ffn_in['bv'], 'L0_ffn_Wo': _L0_ffn_in['Wo'], 'L0_ffn_bo': _L0_ffn_in['bo'], 'L0_ffn_router_w': _L0_ffn_in['router_w'], 'L0_ffn_router_b': _L0_ffn_in['router_b'], 'L0_ffn_W1': _L0_ffn_in['W1'], 'L0_ffn_b1': _L0_ffn_in['b1'], 'L0_ffn_W2': _L0_ffn_in['W2'], 'L0_ffn_b2': _L0_ffn_in['b2'], 'L0_ffn_ln1_g': _L0_ffn_in['ln1_g'], 'L0_ffn_ln1_b': _L0_ffn_in['ln1_b'], 'L0_ffn_ln2_g': _L0_ffn_in['ln2_g'], 'L0_ffn_ln2_b': _L0_ffn_in['ln2_b']}

def reference(x, ctx_1024, cond_1024, L0_xcond_fusion_W, L0_xcond_fusion_b, L0_xcond_ln_gamma, L0_xcond_ln_beta, L0_ffn_Wq, L0_ffn_bq, L0_ffn_Wk, L0_ffn_bk, L0_ffn_Wv, L0_ffn_bv, L0_ffn_Wo, L0_ffn_bo, L0_ffn_router_w, L0_ffn_router_b, L0_ffn_W1, L0_ffn_b1, L0_ffn_W2, L0_ffn_b2, L0_ffn_ln1_g, L0_ffn_ln1_b, L0_ffn_ln2_g, L0_ffn_ln2_b):
    import jax
    import jax.numpy as jnp

    def _L0_xcond_ref(x, fwd_Wz, fwd_bz, fwd_Wh, fwd_bh, bwd_Wz, bwd_bz, bwd_Wh, bwd_bh, fusion_W, fusion_b, ln_gamma, ln_beta):
        import jax, jax.numpy as jnp
        import numpy as np
        B, S, H, L = (4, 256, 128, 4)
        CLAMP_LO, CLAMP_HI = (1e-08, 1.0 - 1e-08)
        LN_EPS = 1e-05

        def _linear_scan(a, b):

            def combine(left, right):
                al, bl = left
                ar, br = right
                return (ar * al, ar * bl + br)
            _, h = jax.lax.associative_scan(combine, (a, b), axis=1)
            return h

        def _mingru(x, Wz, bz, Wh, bh):
            z = jax.nn.sigmoid(jnp.einsum('bsi,hi->bsh', x, Wz) + bz)
            h_tilde = jnp.tanh(jnp.einsum('bsi,hi->bsh', x, Wh) + bh)
            a = jnp.clip(1.0 - z, CLAMP_LO, CLAMP_HI)
            return _linear_scan(a, z * h_tilde)

        def _layernorm(x, gamma, beta):
            mu = jnp.mean(x, axis=-1, keepdims=True)
            var = jnp.mean(jnp.square(x - mu), axis=-1, keepdims=True)
            return (x - mu) * jax.lax.rsqrt(var + LN_EPS) * gamma + beta

        def _stack(x, Wz, bz, Wh, bh, gamma, beta):
            h = x
            for i in range(L):
                h_new = _mingru(h, Wz[i], bz[i], Wh[i], bh[i])
                if i > 0:
                    h_new = h_new + h
                h = _layernorm(h_new, gamma, beta)
            return h
        h_fwd = _stack(x, fwd_Wz, fwd_bz, fwd_Wh, fwd_bh, ln_gamma, ln_beta)
        h_bwd = _stack(jnp.flip(x, axis=1), bwd_Wz, bwd_bz, bwd_Wh, bwd_bh, ln_gamma, ln_beta)
        h_bwd = jnp.flip(h_bwd, axis=1)
        h_comb = jnp.concatenate([h_fwd, h_bwd], axis=-1)
        return jnp.einsum('bsi,hi->bsh', h_comb, fusion_W) + fusion_b

    def _L0_ffn_ref(src, Wq, bq, Wk, bk, Wv, bv, Wo, bo, router_w, router_b, W1, b1, W2, b2, ln1_g, ln1_b, ln2_g, ln2_b):
        import jax, jax.numpy as jnp
        import numpy as np
        D_MODEL = 128
        N_HEAD = 16
        HEAD_DIM = D_MODEL // N_HEAD
        D_FF = 512
        N_EXPERTS = 4
        EPS = 1e-05

        def _layer_norm(x, gamma, beta):
            mu = jnp.mean(x, axis=-1, keepdims=True)
            var = jnp.mean((x - mu) ** 2, axis=-1, keepdims=True)
            return (x - mu) / jnp.sqrt(var + EPS) * gamma + beta
        B, T, _ = src.shape
        q = (src @ Wq + bq).reshape(B, T, N_HEAD, HEAD_DIM)
        k = (src @ Wk + bk).reshape(B, T, N_HEAD, HEAD_DIM)
        v = (src @ Wv + bv).reshape(B, T, N_HEAD, HEAD_DIM)
        scale = HEAD_DIM ** (-0.5)
        scores = jnp.einsum('bqhd,bkhd->bhqk', q, k) * scale
        probs = jax.nn.softmax(scores, axis=-1)
        attn = jnp.einsum('bhqk,bkhd->bqhd', probs, v).reshape(B, T, D_MODEL)
        attn = attn @ Wo + bo
        x = _layer_norm(src + attn, ln1_g, ln1_b)
        keys = (x @ router_w + router_b)[..., 0]
        expert_idx = jnp.remainder(jnp.floor(keys).astype(jnp.int32), N_EXPERTS)
        ff_out = jnp.zeros_like(x)
        for e in range(N_EXPERTS):
            h = jax.nn.relu(x @ W1[e] + b1[e])
            y = h @ W2[e] + b2[e]
            ff_out = ff_out + jnp.where((expert_idx == e)[..., None], y, 0.0)
        return _layer_norm(x + ff_out, ln2_g, ln2_b)
    x = x + _L0_xcond_ref(_layernorm(x, axis=-1), ctx_1024, cond_1024, ctx_1024, cond_1024, ctx_1024, cond_1024, ctx_1024, cond_1024, L0_xcond_fusion_W, L0_xcond_fusion_b, L0_xcond_ln_gamma, L0_xcond_ln_beta)
    x = x + _L0_ffn_ref(_layernorm(x, axis=-1), L0_ffn_Wq, L0_ffn_bq, L0_ffn_Wk, L0_ffn_bk, L0_ffn_Wv, L0_ffn_bv, L0_ffn_Wo, L0_ffn_bo, L0_ffn_router_w, L0_ffn_router_b, L0_ffn_W1, L0_ffn_b1, L0_ffn_W2, L0_ffn_b2, L0_ffn_ln1_g, L0_ffn_ln1_b, L0_ffn_ln2_g, L0_ffn_ln2_b)
    return x

_drawn_inputs = setup_inputs


def setup_inputs(seed=0):
    import zlib

    import numpy as np

    out = dict(_drawn_inputs(seed))
    spreads = {'L0_xcond_ln_gamma': (1.0, 0.2),
     'L0_xcond_ln_beta': (0.0, 0.1),
     'L0_ffn_bq': (0.0, 0.1),
     'L0_ffn_bk': (0.0, 0.8),
     'L0_ffn_bv': (0.0, 0.1),
     'L0_ffn_bo': (0.0, 0.1),
     'L0_ffn_b1': (0.0, 0.331),
     'L0_ffn_b2': (0.0, 0.1),
     'L0_ffn_ln1_g': (1.0, 0.2),
     'L0_ffn_ln1_b': (0.0, 0.1),
     'L0_ffn_ln2_g': (1.0, 0.2),
     'L0_ffn_ln2_b': (0.0, 0.1)}
    factors = {}
    for name, (base, spread) in spreads.items():
        noise = np.random.default_rng([zlib.crc32(name.encode()), seed]).standard_normal(out[name].shape)
        drawn = base * np.exp(spread * noise) if base else spread * noise
        out[name] = jnp.asarray(drawn.astype(out[name].dtype))
    for name, factor in factors.items():
        out[name] = (out[name] * factor).astype(out[name].dtype)
    return out
```

```python
from contextlib import ExitStack

import concourse.bass as bass
from concourse import mybir

F32 = mybir.dt.float32
BF16 = mybir.dt.bfloat16
I32 = mybir.dt.int32
U32 = mybir.dt.uint32
ALU = mybir.AluOpType
ACT = mybir.ActivationFunctionType
AX = mybir.AxisListType

P = 128
CHUNK = 512
TPC = CHUNK // P
LAYERS = 4
NHEAD = 16
HD = P // NHEAD
NE = 4
DFF = 512
FC = DFF // P
EPS = 1e-5
CLAMP_LO, CLAMP_HI = 1e-8, 1.0 - 1e-8
RSQRT_MAGIC = float(0x5F3759DF)
VPITCH = 2048 + 128

R_COND, R_GAMMA, R_BETA, R_FB, R_BQ, R_BK, R_G1, R_B1LN, R_B1 = 0, 4, 5, 6, 7, 8, 9, 10, 11
NVEC = R_B1 + NE * FC

LAG_ROWS, LAG_STATS, LAG_NORM, LAG_COLS, LAG_AFFINE = 2, 3, 4, 5, 6
STEPS = 8


def build(nc, x, ctx_w, cond, fusion_w, fusion_b, ln_gamma, ln_beta, wq, bq, wk, bk, wv, bv, wo, bo,
          router_w, router_b, w1, b1, w2, b2, ln1_g, ln1_b, ln2_g, ln2_b, out):
    B, S, D = x.shape
    NT = B
    NG = NT // TPC
    assert (S, D) == (P, P) and NT % TPC == 0
    SCALE = float(HD) ** -0.5

    with ExitStack() as stack:
        def sb(name, shape, dt=F32):
            return stack.enter_context(nc.sbuf_tensor(name, shape, dt))

        def sem(name):
            return stack.enter_context(nc.semaphore(name))

        bank = [stack.enter_context(nc.psum_tensor(f"bank{i}", [P, 512], F32)) for i in range(8)]

        x_rows = sb("x_rows", [P, NT, P])
        ident = sb("ident", [P, P])
        ident_rw = sb("ident_rw", [P, P + 1])
        ident_bf = sb("ident_bf", [P, P], BF16)
        head16 = sb("head16", [P, NHEAD])
        head_mask = sb("head_mask", [P, 4])
        ctx_rows = sb("ctx_rows", [P, LAYERS, P])
        gate_wT = sb("gate_wT", [P, LAYERS, P + 1])
        gate_cur = sb("gate_cur", [P, P + 1])
        fw_rows = sb("fw_rows", [P, 2, P])
        fwT = sb("fwT", [P, 2, P])
        vec_rows = sb("vec_rows", [NVEC, P])
        vec = sb("vec", [P, NVEC])
        wq_s, wk_s, wv_s, wo_s = (sb(n, [P, P]) for n in ("wq_s", "wk_s", "wv_s", "wo_s"))
        w1_s = sb("w1_s", [P, NE, DFF])
        w2_s = sb("w2_s", [P, NE, FC, P])
        rb_bc = sb("rb_bc", [P, 1])
        bv_bc, bo_bc, g2_bc, b2ln_bc = (sb(n, [P, P]) for n in ("bv_bc", "bo_bc", "g2_bc", "b2ln_bc"))
        b2_blk = sb("b2_blk", [TPC * NE, TPC, P])
        xT = sb("xT", [P, NT * P])
        h = [sb("h_fwd", [P, NT * P]), sb("h_bwd", [P, NT * P])]
        z_and_t = sb("z_and_t", [P, 2, 4, CHUNK])
        z_buf, t_buf = z_and_t[:, 0], z_and_t[:, 1]
        a_buf = [sb("a_fwd", [P, 2, TPC, P]), sb("a_bwd", [P, 2, TPC, P])]
        b_buf = sb("b_buf", [P, 4, CHUNK])
        s_buf = sb("s_buf", [P, 4, CHUNK])
        n_buf = sb("n_buf", [P, 4, TPC, P])
        st = sb("st", [P, 2, 8, 6])
        co = sb("co", [P, 2, 2, 8])
        tmp = sb("tmp", [P, 6, 8])
        fus = sb("fus", [P, CHUNK])
        x1 = sb("x1", [P, TPC, P])
        xn = sb("xn", [P, TPC, P])
        xnb = sb("xnb", [P, TPC, P])
        xnT = sb("xnT", [P, CHUNK])
        q_s = sb("q_s", [P, CHUNK])
        k_s = sb("k_s", [P, CHUNK])
        q_bf = sb("q_bf", [P, CHUNK], BF16)
        q_m = b_buf
        k_m = sb("k_m", [P, 4, CHUNK], BF16)
        v_z = sb("v_z", [P, TPC, VPITCH])
        def v_blocks(off):
            return v_z[:, :, off:off + 8 * 136].rearrange("p t (h y) -> p t h y", y=136)[:, :, :, 0:HD]

        v_dims = (v_blocks(0), v_blocks(1024 + 64))

        def ones_in_v(t):
            return v_blocks(64)[:, t], v_blocks(1024)[:, t]

        mx = sb("mx", [P, 2, NHEAD])
        mneg = sb("mneg", [P, 2, NHEAD], BF16)
        probs = sb("probs", [P, 2, NHEAD, P])
        sums = sb("sums", [P, CHUNK])
        rsums = sb("rsums", [P, CHUNK])
        att = sb("att", [P, CHUNK])
        xh2 = sb("xh2", [P, TPC, P])
        r1 = sb("r1", [P, TPC, P])
        xh = sb("xh", [P, TPC, P])
        xaT = sb("xaT", [P, CHUNK])
        key = sb("key", [P, TPC])
        kf = sb("kf", [P, 4, TPC])
        ki = sb("ki", [P, TPC], I32)
        mask = sb("mask", [P, TPC, NE])
        maskT = sb("maskT", [TPC * NE, P])
        hid = z_and_t
        ym = sb("ym", [P, 2, TPC, P])
        acc = sb("acc", [P, TPC, P])
        x1b = sb("x1b", [P, TPC, P])
        o_s = sb("o_s", [P, TPC, P])

        names = """x_in0 x_in1 x_in2 x_in3 ctx_in vec_in fw_in rw_in attw_in bc_in b2_in w1_in w2_in out_done
        ident_done pool_init mask_done x_norm x_rowsT x_cols prep_T prep_cols
        w_cur u_ready gated decay s_ready rows_ready coef n_dve n_act cols_ready h_ready dve1
        fus_p fus_s fusT_p x1_r xn_r xnT_p xnT_s q_p q_r k_p k_r v_p v_r heads_r xnb_r qbf_r
        sc_p mx_r mneg_r st_p exp_r pv_p sums_r att_r wo_p r1_r xh1_r xh1T_p xaT_s base_p mask_r
        maskT_p maskT_s b2_p hid_p relu_act relu_dve y_p ym_r acc0_r acc_r xh2_r fin_pool o_r dve2""".split()
        s = {n: sem(n) for n in names}
        x_in = [s[f"x_in{i}"] for i in range(NG)]

        def col(r):
            return vec[:, r:r + 1]

        def tiles(ap):
            return ap.rearrange("p (t c) -> p t c", c=P)

        def chunk_of(k):
            c = (k % STEPS) // 2
            return slice(c * CHUNK, (c + 1) * CHUNK)

        class Chain:

            def __init__(self, eng, sm, base=0):
                self.eng, self.sm, self.base, self.n = eng, sm, base, 0

            def mark(self, ins):
                ins.then_inc(self.sm, 1)
                self.n += 1

            def then(self, ins):
                self.mark(ins)
                self.eng.wait_ge(self.sm, self.base + self.n)

        def wait(eng, name, value):
            if not isinstance(value, int) or value > 0:
                eng.wait_ge(s[name], value)

        def token_stats(dve, ch, src, slot, first=0, beside=None):
            for i in range(TPC):
                last = dve.bn_stats(st[:, slot, first + i, :], src(i))
            ch.mark(last)
            if beside:
                beside()
            dve.wait_ge(ch.sm, ch.base + ch.n)

        def coefficients(dve, ch, slot, n):
            even_m, even_v = st[:, slot, 0:n, 1], st[:, slot, 0:n, 2]
            odd_m, odd_v = st[:, slot, 0:n, 4], st[:, slot, 0:n, 5]
            msum, mdif, m2, v, y, w = (tmp[:, i, 0:n] for i in range(6))
            rstd, nmr = co[:, slot, 0, 0:n], co[:, slot, 1, 0:n]
            dve.tensor_tensor(msum, even_m, odd_m, ALU.add)
            dve.tensor_tensor(mdif, even_m, odd_m, ALU.subtract)
            ch.then(dve.scalar_tensor_tensor(out=m2, in0=even_v, scalar=P * EPS, in1=odd_v,
                                             op0=ALU.add, op1=ALU.add))
            ch.then(dve.scalar_tensor_tensor(out=w, in0=mdif, scalar=0.25, in1=mdif,
                                             op0=ALU.mult, op1=ALU.mult))
            ch.then(dve.scalar_tensor_tensor(out=v, in0=m2, scalar=1.0 / P, in1=w,
                                             op0=ALU.mult, op1=ALU.add))
            ch.then(dve.tensor_scalar(w.bitcast(U32), v.bitcast(U32), 1, None, ALU.logical_shift_right))
            ch.then(dve.tensor_scalar(y.bitcast(I32), w.bitcast(I32), -1.0, RSQRT_MAGIC,
                                      ALU.mult, ALU.add))
            for i in range(3):
                ch.then(dve.scalar_tensor_tensor(out=w, in0=y, scalar=-0.5, in1=y,
                                                 op0=ALU.mult, op1=ALU.mult))
                ch.then(dve.tensor_tensor(w, w, v, ALU.mult))
                ch.then(dve.scalar_tensor_tensor(out=rstd if i == 2 else y, in0=w, scalar=1.5, in1=y,
                                                 op0=ALU.add, op1=ALU.mult))
            return dve.scalar_tensor_tensor(out=nmr, in0=msum, scalar=-0.5, in1=rstd,
                                            op0=ALU.mult, op1=ALU.mult)

        COEF_LINKS = 14

        def normalise(dve, dst, src, slot, first=0):
            for i in range(TPC):
                last = dve.tensor_scalar(dst(i), src(i), co[:, slot, 0, first + i:first + i + 1],
                                         co[:, slot, 1, first + i:first + i + 1], ALU.mult, ALU.add)
            return last

        def u_bank(k, layer0):
            return bank[(k // 2) % 2 if layer0 else k % 2]

        def rows_bank(k):
            return bank[2 + k % 4]

        def cols_bank(k):
            return bank[6 + k % 2]

        block = stack.enter_context(nc.Block())

        @block.sync
        def _(sp):
            xr = x.rearrange("b s d -> s b d")
            r = 0
            for v in (cond[0:LAYERS, :], ln_gamma, ln_beta, fusion_b, bq, bk, ln1_g, ln1_b,
                      b1.rearrange("e (c d) -> (e c) d", d=P)):
                v2 = v if len(v.shape) == 2 else v.rearrange("(o d) -> o d", o=1)
                if r == 0:
                    sp.dma_start(x_rows[:, 0:TPC, :], xr[:, 0:TPC, :]).then_inc(x_in[0], 16)
                    sp.dma_start(ctx_rows[:, :, :], ctx_w[0:LAYERS].rearrange("l h i -> h l i")).then_inc(s["ctx_in"], 16)
                sp.dma_start(vec_rows[r:r + v2.shape[0], :], v2).then_inc(s["vec_in"], 16)
                r += v2.shape[0]
            for c in range(1, NG):
                sp.dma_start(x_rows[:, TPC * c:TPC * (c + 1), :], xr[:, TPC * c:TPC * (c + 1), :]).then_inc(x_in[c], 16)
            sp.dma_start(fw_rows[:, :, :], fusion_w.rearrange("h (a i) -> h a i", a=2)).then_inc(s["fw_in"], 16)
            for t, w in ((wq_s, wq), (wk_s, wk), (wv_s, wv), (wo_s, wo)):
                sp.dma_start(t[:, :], w).then_inc(s["attw_in"], 16)
            for t, v in ((bv_bc, bv), (bo_bc, bo), (g2_bc, ln2_g), (b2ln_bc, ln2_b), (rb_bc, router_b)):
                sp.dma_start(t[:, :], v.rearrange("(o d) -> o d", o=1).to_broadcast([P, v.shape[0]])).then_inc(s["bc_in"], 16)
            sp.dma_start(ident_rw[:, P:P + 1], router_w).then_inc(s["rw_in"], 16)
            sp.wait_ge(s["pool_init"], 1)
            for t in range(TPC):
                sp.dma_start(b2_blk[NE * t:NE * t + NE, t, :], b2).then_inc(s["b2_in"], 16)
            sp.dma_start(w1_s[:, :, :], w1.rearrange("e d f -> d e f")).then_inc(s["w1_in"], 16)
            for e in range(NE):
                sp.dma_start(w2_s[:, e, :, :], w2[e].rearrange("(c f) d -> f c d", f=P)).then_inc(s["w2_in"], 16)
            out_v = out.rearrange("b s d -> s b d")
            with sp.Fori(0, NG) as g:
                sp.wait_ge(s["o_r"], g + 1)
                sp.dma_start(out_v[:, bass.ds(g * TPC, TPC), :], o_s[:, :, :]).then_inc(s["out_done"], 16)
            sp.wait_ge(s["out_done"], 16 * NG)

        @block.gpsimd
        def _(pool):
            pool.memset(ident[:, :], 0.0).then_inc(s["ident_done"], 1)
            pool.memset(ident_rw[:, 0:P], 0.0).then_inc(s["ident_done"], 1)
            pool.memset(ident_bf[:, :], 0.0).then_inc(s["ident_done"], 1)
            pool.wait_ge(s["ident_done"], 3)
            for m in (ident[:, :], ident_rw[:, 0:P], ident_bf[:, :]):
                pool.affine_select(out=m, in_=m, compare_op=ALU.not_equal, fill=1.0, base=0,
                                   pattern=[[-1, P]], channel_multiplier=1).then_inc(s["ident_done"], 1)
            pool.memset(b2_blk[:, :, :], 0.0).then_inc(s["pool_init"], 1)
            for d in range(2):
                pool.memset(h[d][:, :], 0.0).then_inc(s["pool_init"], 1)
            pool.memset(a_buf[0][:, :, :, 0:1], 0.0).then_inc(s["pool_init"], 1)
            pool.memset(a_buf[1][:, :, :, P - 1:P], 0.0).then_inc(s["pool_init"], 1)
            for t in range(TPC):
                pool.memset(v_z[:, t, :], 0.0).then_inc(s["pool_init"], 1)
            pool.wait_ge(s["pool_init"], 5 + TPC)
            for t in range(TPC):
                for o in ones_in_v(t):
                    pool.memset(o, 1.0).then_inc(s["pool_init"], 1)

            def decay(l, k, dirs=1):
                n, i = l * STEPS + k, k % 4
                wait(pool, "gated", n + dirs)
                wait(pool, "s_ready", n - 2)
                pool.tensor_tensor(b_buf[:, i, :], z_buf[:, i, :], t_buf[:, i, :],
                                   ALU.mult).then_inc(s["decay"], dirs)
                for d in ((k % 2,) if dirs == 1 else (0, 1)):
                    keep = slice(1, P) if d == 0 else slice(0, P - 1)
                    pool.tensor_scalar(a_buf[d][:, (k // 2) % 2, :, keep], tiles(z_buf[:, i, :])[:, :, keep],
                                       -1.0, 1.0, ALU.mult, ALU.add).then_inc(s["decay"], 1)

            for k in range(0, STEPS, 2):
                decay(0, k, dirs=2)
            with pool.Fori(1, LAYERS) as l:
                for k in range(STEPS):
                    decay(l, k)

            pool.wait_ge(s["bc_in"], 16 * 5)
            pool.wait_ge(s["mask_done"], 1)

            def front(g):
                pool.wait_ge(s["xn_r"], g + 1)
                wait(pool, "r1_r", g)
                pool.wait_ge(s["q_r"], g + 1)
                pool.wait_ge(s["k_r"], g + 1)
                pool.tensor_tensor(xnb[:, :, :], xn[:, :, :], bo_bc[:, :].unsqueeze(1).to_broadcast([P, TPC, P]),
                                   ALU.add).then_inc(s["xnb_r"], 1)
                for src, dst in ((q_s, q_m), (k_s, k_m)):
                    for i in range(4):
                        pool.tensor_scalar(dst[:, i, :], src[:, :], head_mask[:, i:i + 1], 1.0,
                                           ALU.mult, ALU.mult).then_inc(s["heads_r"], 1)

            def finish(g):
                pool.wait_ge(s["acc0_r"], g + 1)
                for e in range(1, NE):
                    pool.wait_ge(s["ym_r"], NE * g + e + 1)
                    pool.tensor_tensor(acc[:, :, :], acc[:, :, :], ym[:, e % 2, :, :],
                                       ALU.add).then_inc(s["acc_r"], 1)
                    if e < NE - 1:
                        pool.wait_ge(s["acc_r"], (NE - 1) * g + e)
                pool.wait_ge(s["x1_r"], g + 1)
                pool.tensor_tensor(x1b[:, :, :], x_rows[:, bass.ds(g * TPC, TPC), :],
                                   b2ln_bc[:, :].unsqueeze(1).to_broadcast([P, TPC, P]),
                                   ALU.add).then_inc(s["fin_pool"], 1)
                pool.wait_ge(s["xh2_r"], g + 1)
                wait(pool, "out_done", 16 * g)
                pool.tensor_tensor(o_s[:, :, :], xh2[:, :, :], g2_bc[:, :].unsqueeze(1).to_broadcast([P, TPC, P]),
                                   ALU.mult).then_inc(s["fin_pool"], 1)
                pool.wait_ge(s["fin_pool"], 2 * g + 2)
                pool.tensor_tensor(o_s[:, :, :], o_s[:, :, :], x1b[:, :, :], ALU.add).then_inc(s["o_r"], 1)

            front(0)
            front(1)
            finish(0)
            with pool.Fori(1, NG - 1) as g:
                front(g + 1)
                finish(g)
            finish(NG - 1)

        @block.tensor
        def _(pe):
            def turn(dst, src, n=P):
                return pe.transpose(dst, src, ident[0:n, 0:n])

            pe.wait_ge(s["ident_done"], 6)
            pe.wait_ge(s["ctx_in"], 16)
            for l in range(LAYERS):
                last = turn(bank[0][:, l * P:(l + 1) * P], ctx_rows[:, l, :])
            last.then_inc(s["prep_T"], 1)
            pe.wait_ge(s["vec_in"], 16 * 9)
            turn(bank[1][:, 0:NVEC], vec_rows[:, :], NVEC).then_inc(s["prep_T"], 1)
            pe.wait_ge(s["fw_in"], 16)
            for a in range(2):
                last = turn(bank[6][:, a * P:(a + 1) * P], fw_rows[:, a, :])
            last.then_inc(s["prep_T"], 1)
            for c in range(NG):
                pe.wait_ge(s["x_norm"], c + 1)
                for t in range(TPC):
                    last = turn(rows_bank(c)[:, t * P:(t + 1) * P], n_buf[:, c, t, :])
                last.then_inc(s["x_rowsT"], 1)

            def gate_in(l, k, layer0=False):
                n = l * STEPS + k
                if layer0:
                    wait(pe, "gated", n - 2)
                    pe.wait_ge(s["x_cols"], k // 2 + 1)
                    pe.matmul(u_bank(k, True)[:, :], gate_wT[:, 0, 0:P], xT[:, chunk_of(k)],
                              start=True, stop=True).then_inc(s["u_ready"], 2)
                    return
                if k == 0:
                    pe.wait_ge(s["w_cur"], l)
                wait(pe, "gated", n - 1)
                wait(pe, "h_ready", n - STEPS + 1)
                pe.matmul(u_bank(k, False)[:, :], gate_cur[:, 0:P], h[k % 2][:, chunk_of(k)],
                          start=True, stop=True).then_inc(s["u_ready"], 1)

            def to_rows(l, k):
                n, m = l * STEPS + k, l * (STEPS // 2) + k // 2
                if isinstance(l, int) and l == 0 and k < 4:
                    pe.wait_ge(s["x_cols"], k + 1)
                wait(pe, "s_ready", n + 1)
                wait(pe, "n_dve" if k % 2 == 0 else "n_act", m - 1)
                src = h[k % 2][:, chunk_of(k)]
                for t in range(TPC):
                    dst = rows_bank(k)[:, t * P:(t + 1) * P]
                    pe.matmul(dst, s_buf[:, k % 4, t * P:(t + 1) * P], ident[:, :], is_transpose=True,
                              start=True, stop=False)
                    last = pe.matmul(dst, src[:, t * P:(t + 1) * P], ident[:, :], is_transpose=True,
                                     start=False, stop=True)
                last.then_inc(s["rows_ready"], 1)

            def to_cols(l, k):
                n, m = l * STEPS + k, l * (STEPS // 2) + k // 2
                wait(pe, "n_dve" if k % 2 == 0 else "n_act", m + 1)
                wait(pe, "h_ready", n - 1)
                for t in range(TPC):
                    last = turn(cols_bank(k)[:, t * P:(t + 1) * P], n_buf[:, k % 4, t, :])
                last.then_inc(s["cols_ready"], 1)

            pe.wait_ge(s["prep_cols"], 3)
            pe.wait_ge(s["pool_init"], 3)
            for k in range(STEPS):
                if k % 2 == 0:
                    gate_in(0, k, layer0=True)
                if k >= LAG_ROWS:
                    to_rows(0, k - LAG_ROWS)
                if k >= LAG_COLS:
                    to_cols(0, k - LAG_COLS)
            with pe.Fori(1, LAYERS) as l:
                for k in range(STEPS):
                    gate_in(l, k)
                    to_rows(l, k - LAG_ROWS)
                    to_cols(l, k - LAG_COLS)
            for k in range(STEPS, STEPS + LAG_COLS):
                if k - LAG_ROWS < STEPS:
                    to_rows(LAYERS - 1, k - LAG_ROWS)
                to_cols(LAYERS - 1, k - LAG_COLS)

            def fusion(g):
                wait(pe, "k_r", g)
                at = bass.ds(g * CHUNK, CHUNK)
                pe.matmul(bank[6][:, :], fwT[:, 0, :], h[0][:, at], start=True, stop=False)
                pe.matmul(bank[6][:, :], fwT[:, 1, :], h[1][:, at], start=False, stop=True).then_inc(s["fus_p"], 1)
                pe.wait_ge(s["fus_s"], g + 1)
                wait(pe, "v_r", g)
                for t in range(TPC):
                    last = turn(bank[7][:, t * P:(t + 1) * P], fus[:, t * P:(t + 1) * P])
                last.then_inc(s["fusT_p"], 1)

            def turn_xn(g):
                pe.wait_ge(s["xn_r"], g + 1)
                wait(pe, "maskT_s", g)
                for t in range(TPC):
                    last = turn(bank[6][:, t * P:(t + 1) * P], xn[:, t, :])
                last.then_inc(s["xnT_p"], 1)

            def queries_keys(g):
                pe.wait_ge(s["xnT_s"], g + 1)
                pe.wait_ge(s["x1_r"], g + 1)
                pe.matmul(bank[7][:, :], wq_s[:, :], xnT[:, :], start=True, stop=True).then_inc(s["q_p"], 1)
                pe.matmul(bank[6][:, :], wk_s[:, :], xnT[:, :], start=True, stop=True).then_inc(s["k_p"], 1)

            def values(g):
                pe.wait_ge(s["q_r"], g + 1)
                for t in range(TPC):
                    last = pe.matmul(bank[7][:, t * P:(t + 1) * P], xnT[:, t * P:(t + 1) * P], wv_s[:, :],
                                     start=True, stop=True)
                last.then_inc(s["v_p"], 1)

            def scores_for_max(g, t):
                for j in range(4):
                    i = NHEAD * g + 4 * t + j
                    if t or j >= 2:
                        pe.wait_ge(s["mx_r"], i - 1)
                    q_t = q_bf[32 * j:32 * j + 32, t * P:(t + 1) * P]
                    k_t = k_m[32 * j:32 * j + 32, :, t * P:(t + 1) * P]
                    pe.matmul(bank[j % 2][:, :], q_t, k_t, start=True, stop=True).then_inc(s["sc_p"], 1)

            def shifted_scores(g, t):
                pe.wait_ge(s["mneg_r"], TPC * g + t + 1)
                for j in range(4):
                    i = NHEAD * g + 4 * t + j
                    if t or j >= 2:
                        pe.wait_ge(s["exp_r"], i - 1)
                    dst = bank[2 + j % 2]
                    k_t = k_s[32 * j:32 * j + 32, t * P:(t + 1) * P]
                    q_t = q_m[32 * j:32 * j + 32, :, t * P:(t + 1) * P]
                    pe.matmul(dst[:, :], k_t, q_t, start=True, stop=False, skip_group_check=True)
                    for i4 in range(4):
                        hh = 4 * j + i4
                        last = pe.matmul(dst[:, i4 * P:(i4 + 1) * P],
                                         mneg[:, t % 2, hh:hh + 1].to_broadcast([P, P]), ident_bf[:, :],
                                         start=False, stop=(i4 == 3), skip_group_check=True)
                    last.then_inc(s["st_p"], 1)

            def weighted_values(g, t):
                pe.wait_ge(s["exp_r"], NHEAD * g + 4 * t + 4)
                for half in range(2):
                    for i in range(8):
                        hh = 8 * half + i
                        last = pe.matmul(bank[4 + half][:, t * P:(t + 1) * P], v_z[:, t, hh * P:(hh + 1) * P],
                                         probs[:, t % 2, hh, :], start=(i == 0), stop=(i == 7))
                last.then_inc(s["pv_p"], 1)

            def attention(g):
                pe.wait_ge(s["qbf_r"], g + 1)
                pe.wait_ge(s["heads_r"], 8 * (g + 1))
                wait(pe, "relu_act", 8 * g)
                wait(pe, "relu_dve", 8 * g)
                scores_for_max(g, 0)
                for t in range(TPC):
                    if t < TPC - 1:
                        scores_for_max(g, t + 1)
                    if t == 0:
                        wait(pe, "ym_r", NE * g)
                    shifted_scores(g, t)
                    if t == 0:
                        pe.wait_ge(s["v_r"], g + 1)
                        wait(pe, "acc0_r", g)
                    if t >= 1:
                        weighted_values(g, t - 1)
                weighted_values(g, TPC - 1)

            def project(g):
                pe.wait_ge(s["att_r"], 2 * g + 2)
                for t in range(TPC):
                    last = pe.matmul(bank[4][:, t * P:(t + 1) * P], att[:, t * P:(t + 1) * P], wo_s[:, :],
                                     start=True, stop=True)
                last.then_inc(s["wo_p"], 1)

            def base_of(b):
                return bank[4 + b][:, 0:260].rearrange("p (t y) -> p t y", y=130)

            def back_to_cols(g):
                pe.wait_ge(s["xh1_r"], g + 1)
                for t in range(TPC):
                    last = turn(bank[5][:, t * P:(t + 1) * P], xh[:, t, :])
                last.then_inc(s["xh1T_p"], 1)

            def router(g):
                pe.wait_ge(s["xaT_s"], g + 1)
                for t in range(TPC):
                    last = pe.matmul(base_of(t // 2)[:, t % 2, 0:P + 1], xaT[:, t * P:(t + 1) * P],
                                     ident_rw[:, 0:P + 1], start=(t % 2 == 0), stop=True, skip_group_check=True)
                last.then_inc(s["base_p"], 1)

            def routed_bias(g):
                pe.wait_ge(s["mask_r"], g + 1)
                turn(bank[6][0:TPC * NE, 0:P], mask[:, :, :].rearrange("p t e -> p (t e)")).then_inc(s["maskT_p"], 1)
                pe.wait_ge(s["maskT_s"], g + 1)
                for b in range(2):
                    last = pe.matmul(base_of(b)[:, :, 0:P], maskT[:, :], b2_blk[:, 2 * b:2 * b + 2, :],
                                     start=False, stop=True, skip_group_check=True)
                last.then_inc(s["b2_p"], 1)

            def hidden(g, e):
                for c in range(FC):
                    m = FC * e + c
                    if m >= 2:
                        pe.wait_ge(s["relu_act" if m % 2 == 0 else "relu_dve"], 8 * g + m // 2)
                    pe.matmul(bank[m % 2][:, :], w1_s[:, e, c * P:(c + 1) * P], xaT[:, :],
                              start=True, stop=True).then_inc(s["hid_p"], 1)

            def expert_out(g, e):
                pe.wait_ge(s["relu_act"], 8 * g + 2 * e + 2)
                pe.wait_ge(s["relu_dve"], 8 * g + 2 * e + 2)
                if e >= 2:
                    pe.wait_ge(s["ym_r"], NE * g + e - 1)
                for t in range(TPC):
                    for c in range(FC):
                        last = pe.matmul(bank[2 + e % 2][:, t * P:(t + 1) * P], hid[:, e % 2, c, t * P:(t + 1) * P],
                                         w2_s[:, e, c, :], start=(c == 0), stop=(c == FC - 1))
                last.then_inc(s["y_p"], 1)

            def group(g, more):
                attention(g)
                project(g)
                if more:
                    fusion(g + 1)
                back_to_cols(g)
                router(g)
                hidden(g, 0)
                routed_bias(g)
                if more:
                    turn_xn(g + 1)
                hidden(g, 1)
                expert_out(g, 0)
                if more:
                    queries_keys(g + 1)
                hidden(g, 2)
                expert_out(g, 1)
                if more:
                    values(g + 1)
                hidden(g, 3)
                expert_out(g, 2)
                expert_out(g, 3)

            pe.wait_ge(s["h_ready"], LAYERS * STEPS)
            fusion(0)
            turn_xn(0)
            pe.wait_ge(s["attw_in"], 64)
            queries_keys(0)
            values(0)
            for name, v in (("w1_in", 16), ("w2_in", 64), ("b2_in", 64), ("rw_in", 16), ("pool_init", 5 + 3 * TPC)):
                pe.wait_ge(s[name], v)
            group(0, True)
            with pe.Fori(1, NG - 1) as g:
                group(g, True)
            group(NG - 1, False)

        @block.scalar
        def _(act):
            act.wait_ge(s["prep_T"], 1)
            act.activation(gate_wT[:, :, 0:P], tiles(bank[0][:, :]), ACT.Identity).then_inc(s["prep_cols"], 1)
            act.wait_ge(s["prep_T"], 2)
            act.activation(vec[:, :], bank[1][:, 0:NVEC], ACT.Identity)
            act.activation(gate_wT[:, :, P], bank[1][:, R_COND:R_COND + LAYERS], ACT.Identity).then_inc(s["prep_cols"], 1)
            act.wait_ge(s["prep_T"], 3)
            act.activation(fwT[:, :, :], bank[6][:, 0:2 * P].rearrange("p (a h) -> p a h", a=2),
                           ACT.Identity).then_inc(s["prep_cols"], 1)
            for c in range(NG):
                act.wait_ge(s["x_rowsT"], c + 1)
                act.activation(xT[:, c * CHUNK:(c + 1) * CHUNK], rows_bank(c)[:, :], ACT.Identity).then_inc(s["x_cols"], 1)
            act.wait_ge(s["prep_cols"], 3)

            def gates(l, k, layer0=False):
                n, i = l * STEPS + k, k % 4
                dirs = 2 if layer0 else 1
                wait(act, "u_ready", n + dirs)
                wait(act, "decay", 2 * (n - 2))
                src = u_bank(k, layer0)[:, :]
                bias = gate_wT[:, 0, P:P + 1] if layer0 else gate_cur[:, P:P + 1]
                act.activation(z_buf[:, i, :], src, ACT.Sigmoid, bias=bias)
                act.activation(t_buf[:, i, :], src, ACT.Tanh, bias=bias).then_inc(s["gated"], dirs)

            def norm(l, k):
                n, m = l * STEPS + k, l * (STEPS // 2) + k // 2
                slot = (k // 2) % 2
                wait(act, "coef", m + 1)
                wait(act, "cols_ready", n - 3)
                for t in range(TPC):
                    last = act.activation(n_buf[:, k % 4, t, :], rows_bank(k)[:, t * P:(t + 1) * P], ACT.Identity,
                                          scale=co[:, slot, 0, TPC + t:TPC + t + 1],
                                          bias=co[:, slot, 1, TPC + t:TPC + t + 1])
                last.then_inc(s["n_act"], 1)

            def affine(l, k):
                wait(act, "cols_ready", l * STEPS + k + 1)
                act.activation(h[k % 2][:, chunk_of(k)], cols_bank(k)[:, :], ACT.Identity,
                               scale=col(R_GAMMA), bias=col(R_BETA)).then_inc(s["h_ready"], 1)

            def slot1(l, k, first=0, last=STEPS):
                if k % 2 == 0 and first <= k - LAG_NORM + 1 < last:
                    norm(l, k - LAG_NORM + 1)
                if first <= k - LAG_AFFINE < last:
                    affine(l, k - LAG_AFFINE)

            for k in range(STEPS):
                if k % 2 == 0:
                    gates(0, k, layer0=True)
                slot1(0, k)
            with act.Fori(1, LAYERS) as l:
                act.wait_ge(s["u_ready"], l * STEPS)
                act.wait_ge(s["gated"], l * STEPS)
                act.activation(gate_cur[:, :], gate_wT[:, bass.ds(l, 1), :].rearrange("p o c -> p (o c)"),
                               ACT.Identity).then_inc(s["w_cur"], 1)
                act.wait_ge(s["w_cur"], l)
                for k in range(STEPS):
                    gates(l, k)
                    slot1(l, k, first=-STEPS)
            for k in range(STEPS, STEPS + LAG_AFFINE):
                slot1(LAYERS - 1, k)

            def fusion(g):
                act.wait_ge(s["fus_p"], g + 1)
                act.activation(fus[:, :], bank[6][:, :], ACT.Identity, bias=col(R_FB)).then_inc(s["fus_s"], 1)

            def xn_cols(g):
                act.wait_ge(s["xnT_p"], g + 1)
                act.activation(xnT[:, :], bank[6][:, :], ACT.Identity).then_inc(s["xnT_s"], 1)

            def queries_keys(g):
                act.wait_ge(s["q_p"], g + 1)
                wait(act, "heads_r", 8 * g)
                act.activation(q_s[:, :], bank[7][:, :], ACT.Identity, bias=col(R_BQ)).then_inc(s["q_r"], 1)
                act.wait_ge(s["k_p"], g + 1)
                act.activation(k_s[:, :], bank[6][:, :], ACT.Identity, bias=col(R_BK)).then_inc(s["k_r"], 1)
                act.wait_ge(s["q_r"], g + 1)
                act.activation(q_bf[:, :], q_s[:, :], ACT.Identity).then_inc(s["qbf_r"], 1)

            def attention(g):
                for t in range(TPC):
                    if t < 2:
                        wait(act, "pv_p", TPC * g)
                    else:
                        act.wait_ge(s["pv_p"], TPC * g + t - 1)
                    for j in range(4):
                        act.wait_ge(s["st_p"], NHEAD * g + 4 * t + j + 1)
                        act.activation(probs[:, t % 2, 4 * j:4 * j + 4, :], tiles(bank[2 + j % 2][:, :]), ACT.Exp,
                                       scale=SCALE).then_inc(s["exp_r"], 1)
                act.wait_ge(s["pv_p"], TPC * g + TPC)
                act.activation(sums[64:128, :], bank[4][64:128, :], ACT.Identity).then_inc(s["sums_r"], 1)
                act.activation(sums[0:64, :], bank[5][0:64, :], ACT.Identity).then_inc(s["sums_r"], 1)

            def xa_cols(g):
                act.wait_ge(s["xh1T_p"], g + 1)
                act.activation(xaT[:, :], bank[5][:, :], ACT.Identity, scale=col(R_G1),
                               bias=col(R_B1LN)).then_inc(s["xaT_s"], 1)

            def relu(g, e):
                for c in range(0, FC, 2):
                    m = FC * e + c
                    act.wait_ge(s["hid_p"], NE * FC * g + m + 1)
                    act.activation(hid[:, e % 2, c, :], bank[0][:, :], ACT.Relu,
                                   bias=col(R_B1 + m)).then_inc(s["relu_act"], 1)

            def mask_rows(g):
                act.wait_ge(s["maskT_p"], g + 1)
                act.activation(maskT[:, :], bank[6][0:TPC * NE, 0:P], ACT.Identity).then_inc(s["maskT_s"], 1)

            def group(g, more):
                attention(g)
                if more:
                    fusion(g + 1)
                xa_cols(g)
                relu(g, 0)
                mask_rows(g)
                if more:
                    xn_cols(g + 1)
                relu(g, 1)
                if more:
                    queries_keys(g + 1)
                relu(g, 2)
                relu(g, 3)

            fusion(0)
            xn_cols(0)
            queries_keys(0)
            group(0, True)
            with act.Fori(1, NG - 1) as g:
                group(g, True)
            group(NG - 1, False)

        @block.vector
        def _(dve):
            ch = Chain(dve, s["dve1"])
            for c in range(NG):
                dve.wait_ge(x_in[c], 16)
                token_stats(dve, ch, lambda i: x_rows[:, TPC * c + i, :], c % 2)
                ch.then(coefficients(dve, ch, c % 2, TPC))
                normalise(dve, lambda i: n_buf[:, c, i, :], lambda i: x_rows[:, TPC * c + i, :],
                          c % 2).then_inc(s["x_norm"], 1)
            dve.wait_ge(s["ident_done"], 6)
            ch.then(dve.reduce_sum(head16[:, :], ident[:, :].rearrange("p (g x) -> p g x", x=HD), AX.X))
            dve.reduce_sum(head_mask[:, :], head16[:, :].rearrange("p (j i) -> p i j", i=4),
                           AX.X).then_inc(s["mask_done"], 1)
            dve.wait_ge(s["pool_init"], 5)

            def scan(ch, l, k, layer0=False):
                n = l * STEPS + k
                d, i = k % 2, ((k - k % 2) if layer0 else k) % 4
                a = a_buf[d][:, (k // 2) % 2, :, :]
                keep = slice(1, P) if d == 0 else slice(0, P - 1)
                wait(dve, "decay", 2 * (n + (2 if layer0 and d == 0 else 1)))
                ch.then(dve.tensor_scalar(a[:, :, keep], a[:, :, keep], CLAMP_LO, CLAMP_HI, ALU.max, ALU.min))
                wait(dve, "rows_ready", n - 3)
                a = a.rearrange("p t c -> p (t c)")
                b, out_s = b_buf[:, i, :], s_buf[:, k % 4, :]
                if d:
                    a, b, out_s = a[:, ::-1], b[:, ::-1], out_s[:, ::-1]
                dve.tensor_tensor_scan(out_s, a, b, 0.0, ALU.mult, ALU.add).then_inc(s["s_ready"], 1)

            def stats(ch, l, k):
                wait(dve, "rows_ready", l * STEPS + k + 1)
                token_stats(dve, ch, lambda i: rows_bank(k)[:, i * P:(i + 1) * P], (k // 2) % 2, TPC * (k % 2))

            def norm(ch, l, k):
                n, m = l * STEPS + k, l * (STEPS // 2) + k // 2
                slot = (k // 2) % 2
                wait(dve, "n_act", m - 1)
                coefficients(dve, ch, slot, 2 * TPC).then_inc(s["coef"], 1)
                wait(dve, "coef", m + 1)
                wait(dve, "cols_ready", n - 3)
                normalise(dve, lambda i: n_buf[:, k % 4, i, :], lambda i: rows_bank(k)[:, i * P:(i + 1) * P],
                          slot).then_inc(s["n_dve"], 1)

            def slot1(ch, l, k, first=0, last=STEPS):
                if first <= k - LAG_STATS < last:
                    stats(ch, l, k - LAG_STATS)
                if k % 2 == 0 and first <= k - LAG_NORM < last:
                    norm(ch, l, k - LAG_NORM)

            for k in range(STEPS):
                slot1(ch, 0, k)
                scan(ch, 0, k, layer0=True)
            PER_LAYER = 2 * STEPS + (STEPS // 2) * COEF_LINKS
            before = ch.n
            with dve.Fori(1, LAYERS) as l:
                ch = Chain(dve, s["dve1"], (l - 1) * PER_LAYER + before)
                for k in range(STEPS):
                    slot1(ch, l, k, first=-STEPS)
                    scan(ch, l, k)
                assert ch.n == PER_LAYER
            ch = Chain(dve, s["dve1"], before + (LAYERS - 1) * PER_LAYER)
            for k in range(STEPS, STEPS + LAG_NORM):
                slot1(ch, LAYERS - 1, k)

            def front_rows(ch, g):
                dve.wait_ge(s["fusT_p"], g + 1)
                x_g = x_rows[:, bass.ds(g * TPC, TPC), :]
                ch.then(dve.tensor_tensor(x1[:, :, :], tiles(bank[7][:, :]), x_g, ALU.add))
                token_stats(dve, ch, lambda i: x1[:, i, :], 0,
                            beside=lambda: dve.tensor_copy(x_g, x1[:, :, :]).then_inc(s["x1_r"], 1))
                ch.then(coefficients(dve, ch, 0, TPC))
                wait(dve, "xnb_r", g)
                normalise(dve, lambda i: xn[:, i, :], lambda i: x1[:, i, :], 0).then_inc(s["xn_r"], 1)

            def value_rows(g):
                dve.wait_ge(s["v_p"], g + 1)
                for half, dst in enumerate(v_dims):
                    at = slice(64 * half, 64 * half + 64)
                    src = tiles(bank[7][:, :])[:, :, at].rearrange("p t (h y) -> p t h y", y=HD)
                    bias = bv_bc[:, at].rearrange("p (h y) -> p h y", y=HD).unsqueeze(1).to_broadcast([P, TPC, 8, HD])
                    last = dve.tensor_tensor(dst, src, bias, ALU.add)
                last.then_inc(s["v_r"], 1)

            def attention(ch, g):
                for t in range(TPC):
                    for j in range(4):
                        dve.wait_ge(s["sc_p"], NHEAD * g + 4 * t + j + 1)
                        dve.reduce_max(mx[:, t % 2, 4 * j:4 * j + 4], tiles(bank[j % 2][:, :]),
                                       AX.X).then_inc(s["mx_r"], 1)
                    dve.wait_ge(s["mx_r"], NHEAD * g + 4 * t + 4)
                    if t < 2:
                        wait(dve, "st_p", NHEAD * g)
                    else:
                        dve.wait_ge(s["st_p"], NHEAD * g + 4 * t - 4)
                    dve.tensor_scalar(mneg[:, t % 2, :], mx[:, t % 2, :], -1.0, None, ALU.mult).then_inc(s["mneg_r"], 1)
                dve.wait_ge(s["sums_r"], 2 * g + 2)
                ch.then(dve.reciprocal(rsums[:, :], sums[:, :]))
                wait(dve, "wo_p", g)
                dve.tensor_tensor(att[0:64, :], bank[4][0:64, :], rsums[64:128, :], ALU.mult).then_inc(s["att_r"], 1)
                dve.tensor_tensor(att[64:128, :], bank[5][64:128, :], rsums[0:64, :], ALU.mult).then_inc(s["att_r"], 1)

            def first_norm(ch, g):
                dve.wait_ge(s["wo_p"], g + 1)
                dve.wait_ge(s["xnb_r"], g + 1)
                dve.tensor_tensor(r1[:, :, :], tiles(bank[4][:, :]), xnb[:, :, :], ALU.add).then_inc(s["r1_r"], 1)
                dve.wait_ge(s["r1_r"], g + 1)
                token_stats(dve, ch, lambda i: r1[:, i, :], 0)
                ch.then(coefficients(dve, ch, 0, TPC))
                wait(dve, "xh1T_p", g)
                normalise(dve, lambda i: xh[:, i, :], lambda i: r1[:, i, :], 0).then_inc(s["xh1_r"], 1)

            def floor(ch, dst, src, flag):
                ch.then(dve.tensor_copy(ki[:, :], src))
                ch.then(dve.tensor_copy(dst, ki[:, :]))
                ch.then(dve.tensor_tensor(flag, dst, src, ALU.is_gt))
                ch.then(dve.tensor_tensor(dst, dst, flag, ALU.subtract))

            def route(ch, g):
                dve.wait_ge(s["base_p"], g + 1)
                for b in range(2):
                    last = dve.tensor_scalar(key[:, 2 * b:2 * b + 2], bank[4 + b][:, P:P + 131:130], rb_bc[:, :], None,
                                             ALU.add)
                ch.then(last)
                fl, quarter, fq, flag = (kf[:, i, :] for i in range(4))
                floor(ch, fl, key[:, :], flag)
                ch.then(dve.tensor_scalar(quarter, fl, 1.0 / NE, None, ALU.mult))
                floor(ch, fq, quarter, flag)
                ch.then(dve.scalar_tensor_tensor(out=fl, in0=fq, scalar=-float(NE), in1=fl, op0=ALU.mult, op1=ALU.add))
                wait(dve, "maskT_p", g)
                for e in range(NE):
                    last = dve.tensor_scalar(mask[:, :, e], fl, float(e), None, ALU.is_equal)
                last.then_inc(s["mask_r"], 1)

            ROUTE_LINKS = 1 + 4 + 1 + 4 + 1

            def relu(g, e):
                for c in range(1, FC, 2):
                    m = FC * e + c
                    dve.wait_ge(s["hid_p"], NE * FC * g + m + 1)
                    dve.tensor_scalar(hid[:, e % 2, c, :], bank[1][:, :], col(R_B1 + m), 0.0,
                                      ALU.add, ALU.max).then_inc(s["relu_dve"], 1)

            def masked(g, e):
                dve.wait_ge(s["y_p"], NE * g + e + 1)
                if e == 3:
                    dve.wait_ge(s["acc_r"], 3 * g + 1)
                elif e < 2:
                    wait(dve, "acc_r", 3 * g)
                dve.tensor_tensor(ym[:, e % 2, :, :], tiles(bank[2 + e % 2][:, :]),
                                  mask[:, :, e:e + 1].to_broadcast([P, TPC, P]), ALU.mult).then_inc(s["ym_r"], 1)
                if e == 0:
                    dve.wait_ge(s["ym_r"], NE * g + 1)
                    dve.wait_ge(s["b2_p"], g + 1)
                    for b in range(2):
                        last = dve.tensor_tensor(acc[:, 2 * b:2 * b + 2, :], ym[:, 0, 2 * b:2 * b + 2, :],
                                                 bank[4 + b][:, 0:260].rearrange("p (t y) -> p t y", y=130)[:, :, 0:P],
                                                 ALU.add)
                    last.then_inc(s["acc0_r"], 1)

            def second_norm(ch, g):
                dve.wait_ge(s["acc_r"], 3 * g + 3)
                token_stats(dve, ch, lambda i: acc[:, i, :], 0)
                ch.then(coefficients(dve, ch, 0, TPC))
                wait(dve, "o_r", g)
                normalise(dve, lambda i: xh2[:, i, :], lambda i: acc[:, i, :], 0).then_inc(s["xh2_r"], 1)

            def group(ch, g, more):
                attention(ch, g)
                first_norm(ch, g)
                if more:
                    front_rows(ch, g + 1)
                route(ch, g)
                relu(g, 0)
                relu(g, 1)
                masked(g, 0)
                relu(g, 2)
                masked(g, 1)
                if more:
                    value_rows(g + 1)
                relu(g, 3)
                masked(g, 2)
                masked(g, 3)
                second_norm(ch, g)

            NORM_LINKS = COEF_LINKS + 2
            ch = Chain(dve, s["dve2"])
            front_rows(ch, 0)
            dve.wait_ge(s["pool_init"], 5 + 3 * TPC)
            dve.wait_ge(s["bc_in"], 16 * 5)
            value_rows(0)
            before = ch.n
            PER_GROUP = 3 * NORM_LINKS + 1 + 1 + ROUTE_LINKS
            group(ch, 0, True)
            assert ch.n == PER_GROUP + before
            with dve.Fori(1, NG - 1) as g:
                ch = Chain(dve, s["dve2"], g * PER_GROUP + before)
                group(ch, g, True)
                assert ch.n == PER_GROUP
            group(Chain(dve, s["dve2"], before + (NG - 1) * PER_GROUP), NG - 1, False)


_P = "L0_ffn_"
_INS = ["x", "ctx_1024", "cond_1024", "L0_xcond_fusion_W", "L0_xcond_fusion_b", "L0_xcond_ln_gamma",
        "L0_xcond_ln_beta"] + [_P + n for n in (
            "Wq", "bq", "Wk", "bk", "Wv", "bv", "Wo", "bo", "router_w", "router_b", "W1", "b1", "W2", "b2",
            "ln1_g", "ln1_b", "ln2_g", "ln2_b")]


def kernel(**inputs):
    import numpy as _np
    import concourse.bacc as _bacc
    from concourse import mybir as _mybir
    from concourse.bass_utils import run_bass_kernel_spmd as _run

    nc = _bacc.Bacc("TRN2", target_bir_lowering=False, num_devices=1)
    arrays, args = {}, []
    for name in _INS:
        a = _np.ascontiguousarray(inputs[name])
        arrays[f"in_{name}_dram"] = a
        args.append(nc.dram_tensor(f"in_{name}_dram", a.shape, _mybir.dt.from_np(a.dtype), kind="ExternalInput").ap())
    shape = _np.shape(inputs["x"])
    args.append(nc.dram_tensor("out_dram", shape, _mybir.dt.float32, kind="ExternalOutput").ap())
    build(nc, *args)
    r = _run(nc, [arrays], core_ids=[0])
    return r.results[0]["out_dram"]
```

```python
from contextlib import ExitStack

import concourse.bass as bass
from concourse import mybir

F32 = mybir.dt.float32
BF16 = mybir.dt.bfloat16
I32 = mybir.dt.int32
U32 = mybir.dt.uint32
ALU = mybir.AluOpType
ACT = mybir.ActivationFunctionType
AX = mybir.AxisListType

P = 128
CHUNK = 512
TPC = CHUNK // P
LAYERS = 4
NHEAD = 16
HD = P // NHEAD
NE = 4
DFF = 512
FC = DFF // P
EPS = 1e-5
CLAMP_LO, CLAMP_HI = 1e-8, 1.0 - 1e-8
RSQRT_MAGIC = float(0x5F1FFF77)
RSQRT_STEPS = ((0.7038757896311395, 1.6818510386049268), (0.50000015752812, 1.5000004725843))
VPITCH = 2048 + 128

R_COND, R_GAMMA, R_BETA, R_FB, R_BQ, R_BK, R_G1, R_B1LN, R_B1 = 0, 4, 5, 6, 7, 8, 9, 10, 11
NVEC = R_B1 + NE * FC

STEPS = 8
PAIRS = STEPS // 2


def build(nc, x, ctx_w, cond, fusion_w, fusion_b, ln_gamma, ln_beta, wq, bq, wk, bk, wv, bv, wo, bo,
          router_w, router_b, w1, b1, w2, b2, ln1_g, ln1_b, ln2_g, ln2_b, out):
    B, S, D = x.shape
    NT = B
    NG = NT // TPC
    assert (S, D) == (P, P) and NT % TPC == 0
    SCALE = float(HD) ** -0.5

    with ExitStack() as stack:
        def sb(name, shape, dt=F32):
            return stack.enter_context(nc.sbuf_tensor(name, shape, dt))

        def sem(name):
            return stack.enter_context(nc.semaphore(name))

        bank = [stack.enter_context(nc.psum_tensor(f"bank{i}", [P, 512], F32)) for i in range(8)]

        x_rows = sb("x_rows", [P, NT, P])
        ident = sb("ident", [P, P])
        rw_s = sb("rw_s", [P, 1])
        ident_bf = sb("ident_bf", [P, P], BF16)
        head_mask = sb("head_mask", [P, NHEAD])
        ctx_rows = sb("ctx_rows", [P, LAYERS, P])
        gate_wT = sb("gate_wT", [P, LAYERS, P + 1])
        gate_cur = sb("gate_cur", [P, P + 1])
        fw_rows = sb("fw_rows", [P, 2, P])
        fwT = sb("fwT", [P, 2, P])
        vec_rows = sb("vec_rows", [NVEC, P])
        vec = sb("vec", [P, NVEC])
        wq_s, wk_s, wv_s, wo_s = (sb(n, [P, P]) for n in ("wq_s", "wk_s", "wv_s", "wo_s"))
        w1_s = sb("w1_s", [P, NE, DFF])
        w2_s = sb("w2_s", [P, NE, FC, P])
        rb_bc = sb("rb_bc", [P, 1])
        bv_bc, bo_bc, g2_bc, b2ln_bc = (sb(n, [P, P]) for n in ("bv_bc", "bo_bc", "g2_bc", "b2ln_bc"))
        b2_blk = sb("b2_blk", [TPC * NE, TPC, P])
        h = [sb("h_fwd", [P, NT * P]), sb("h_bwd", [P, NT * P])]
        z_and_t = sb("z_and_t", [P, 2, 4, CHUNK])
        z_buf, t_buf = z_and_t[:, 0], z_and_t[:, 1]
        a_buf = [sb("a_fwd", [P, 2, TPC, P]), sb("a_bwd", [P, 2, TPC, P])]
        work = sb("work", [P, NHEAD, CHUNK])
        b_buf, s_buf = work[:, 0:4, :], work[:, 4:8, :]
        n_buf = work[:, 8:12, :].rearrange("p k (t c) -> p k t c", c=P)
        xT = work[:, 12:16, :].rearrange("p k c -> p (k c)")
        st = sb("st", [P, 2, 8, 6])
        co = sb("co", [P, 2, 2, 8])
        tmp = sb("tmp", [P, 6, 8])
        fus = sb("fus", [P, CHUNK])
        x1 = sb("x1", [P, TPC, P])
        xn = sb("xn", [P, TPC, P])
        xnb = sb("xnb", [P, TPC, P])
        xnT = sb("xnT", [P, CHUNK])
        q_s = sb("q_s", [P, CHUNK])
        k_s = sb("k_s", [P, CHUNK])
        q_bf = sb("q_bf", [P, CHUNK], BF16)
        k_bf = sb("k_bf", [P, CHUNK], BF16)
        q_m = work
        k_m = sb("k_m", [P, NHEAD, CHUNK], BF16)
        v_z = sb("v_z", [P, TPC, VPITCH])
        def v_blocks(off):
            return v_z[:, :, off:off + 8 * 136].rearrange("p t (h y) -> p t h y", y=136)[:, :, :, 0:HD]

        v_dims = (v_blocks(0), v_blocks(1024 + 64))

        def ones_in_v(t):
            return v_blocks(64)[:, t], v_blocks(1024)[:, t]

        mx = sb("mx", [P, 2, NHEAD])
        mneg = sb("mneg", [P, 2, NHEAD], BF16)
        probs = sb("probs", [P, 2, NHEAD, P])
        sums = sb("sums", [P, 2, P])
        rsums = sb("rsums", [P, 2, P])
        att = sb("att", [P, CHUNK])
        xh2 = sb("xh2", [P, TPC, P])
        r1 = sb("r1", [P, TPC, P])
        xh = sb("xh", [P, TPC, P])
        xaT = sb("xaT", [P, CHUNK])
        key = sb("key", [P, TPC])
        kf = sb("kf", [P, 4, TPC])
        ki = sb("ki", [P, TPC], I32)
        mask = sb("mask", [P, TPC, NE])
        maskT = fw_rows[0:TPC * NE, 0, :]
        hid = z_and_t
        ym = a_buf[0]
        acc, x1b = a_buf[1][:, 0], a_buf[1][:, 1]
        o_s = ctx_rows

        names = """x_in0 x_in1 x_in2 x_in3 ctx_in vec_in fw_in rw_in attw_in bc_in b2_in w1_in w2_in out_done
        ident_done pool_init mask_done x_norm x_rowsT x_cols prep_T prep_cols
        w_cur u_ready gated decay s_ready rows_ready coef n_dve n_act cols_ready h_ready dve1
        fus_p fus_s fusT_p x1_r xn_r xnT_p xnT_s q_p q_r k_p k_r v_p v_r q_heads_r k_heads_r xnb_r qbf_r kbf_r
        sc_p mx_r mneg_r st_p exp_r pv_p sums_r att_r wo_p r1_r xh1_r xh1T_p xaT_s key_p mask_r
        maskT_p maskT_s b2_p hid_p relu_r y_p ym_r acc0_r acc_r xh2_r fin_pool o_r dve2""".split()
        s = {n: sem(n) for n in names}
        x_in = [s[f"x_in{i}"] for i in range(NG)]

        def col(r):
            return vec[:, r:r + 1]

        def tiles(ap):
            return ap.rearrange("p (t c) -> p t c", c=P)

        def chunk_of(k):
            c = (k % STEPS) // 2
            return slice(c * CHUNK, (c + 1) * CHUNK)

        class Chain:

            def __init__(self, eng, sm, base=0):
                self.eng, self.sm, self.base, self.n = eng, sm, base, 0

            def mark(self, ins):
                ins.then_inc(self.sm, 1)
                self.n += 1

            def then(self, ins):
                self.mark(ins)
                self.eng.wait_ge(self.sm, self.base + self.n)

        def wait(eng, name, value):
            if not isinstance(value, int) or value > 0:
                eng.wait_ge(s[name], value)

        def token_stats(dve, ch, src, slot, first=0, between=None):
            for i in range(TPC):
                last = dve.bn_stats(st[:, slot, first + i, :], src(i))
                if i == TPC - 1:
                    ch.mark(last)
                if between:
                    between()

        class Coefficients:

            LINKS = 12

            def __init__(self, dve, ch, slot, n, at=0):
                self.dve, self.ch, self.i = dve, ch, at
                self.before = ch.n
                self.mean_var = [st[:, slot, 0:n, j] for j in (1, 2, 4, 5)]
                self.tmp = [tmp[:, j, 0:n] for j in range(6)]
                self.rstd, self.nmr = co[:, slot, 0, 0:n], co[:, slot, 1, 0:n]

            def next(self, links=1):
                for _ in range(links):
                    ins = self.link(self.i)
                    self.i += 1
                    if self.i == self.LINKS:
                        return ins
                    self.ch.mark(ins)
                    self.before = self.ch.n

            def finish(self):
                return self.next(self.LINKS - self.i)

            def link(self, i):
                dve = self.dve
                even_m, even_v, odd_m, odd_v = self.mean_var
                msum, mdif, m2, v, y, w = self.tmp
                dve.wait_ge(self.ch.sm, self.ch.base + self.before)
                if i == 0:
                    dve.tensor_tensor(msum, even_m, odd_m, ALU.add)
                    dve.tensor_tensor(mdif, even_m, odd_m, ALU.subtract)
                    return dve.scalar_tensor_tensor(out=m2, in0=even_v, scalar=P * EPS, in1=odd_v,
                                                    op0=ALU.add, op1=ALU.add)
                if i == 1:
                    return dve.scalar_tensor_tensor(out=w, in0=mdif, scalar=0.25, in1=mdif,
                                                    op0=ALU.mult, op1=ALU.mult)
                if i == 2:
                    return dve.scalar_tensor_tensor(out=v, in0=m2, scalar=1.0 / P, in1=w,
                                                    op0=ALU.mult, op1=ALU.add)
                if i == 3:
                    return dve.tensor_scalar(w.bitcast(U32), v.bitcast(U32), 1, None, ALU.logical_shift_right)
                if i == 4:
                    return dve.tensor_scalar(y.bitcast(I32), w.bitcast(I32), -1.0, RSQRT_MAGIC,
                                             ALU.mult, ALU.add)
                if i < 11:
                    step, j = divmod(i - 5, 3)
                    half, one_and_half = RSQRT_STEPS[step]
                    if j == 0:
                        return dve.scalar_tensor_tensor(out=w, in0=y, scalar=-half, in1=y,
                                                        op0=ALU.mult, op1=ALU.mult)
                    if j == 1:
                        return dve.tensor_tensor(w, w, v, ALU.mult)
                    return dve.scalar_tensor_tensor(out=self.rstd if step else y, in0=w, scalar=one_and_half,
                                                    in1=y, op0=ALU.add, op1=ALU.mult)
                return dve.scalar_tensor_tensor(out=self.nmr, in0=msum, scalar=-0.5, in1=self.rstd,
                                                op0=ALU.mult, op1=ALU.mult)

        def normalise(dve, dst, src, slot, first=0, between=None):
            for i in range(TPC):
                last = dve.tensor_scalar(dst(i), src(i), co[:, slot, 0, first + i:first + i + 1],
                                         co[:, slot, 1, first + i:first + i + 1], ALU.mult, ALU.add)
                if between and i < TPC - 1:
                    between()
            return last

        def u_bank(k, layer0):
            return bank[(k // 2) % 2 if layer0 else k % 2]

        def rows_bank(k):
            return bank[2 + k % 4]

        def cols_bank(k):
            return bank[6 + k % 2]

        block = stack.enter_context(nc.Block())

        @block.sync
        def _(sp):
            xr = x.rearrange("b s d -> s b d")
            r = 0
            for v in (cond[0:LAYERS, :], ln_gamma, ln_beta, fusion_b, bq, bk, ln1_g, ln1_b,
                      b1.rearrange("e (c d) -> (e c) d", d=P)):
                v2 = v if len(v.shape) == 2 else v.rearrange("(o d) -> o d", o=1)
                if r == 0:
                    sp.dma_start(x_rows[:, 0:TPC, :], xr[:, 0:TPC, :]).then_inc(x_in[0], 16)
                    sp.dma_start(ctx_rows[:, :, :], ctx_w[0:LAYERS].rearrange("l h i -> h l i")).then_inc(s["ctx_in"], 16)
                sp.dma_start(vec_rows[r:r + v2.shape[0], :], v2).then_inc(s["vec_in"], 16)
                r += v2.shape[0]
            for c in range(1, NG):
                sp.dma_start(x_rows[:, TPC * c:TPC * (c + 1), :], xr[:, TPC * c:TPC * (c + 1), :]).then_inc(x_in[c], 16)
            sp.dma_start(fw_rows[:, :, :], fusion_w.rearrange("h (a i) -> h a i", a=2)).then_inc(s["fw_in"], 16)
            for t, w in ((wq_s, wq), (wk_s, wk), (wv_s, wv), (wo_s, wo)):
                sp.dma_start(t[:, :], w).then_inc(s["attw_in"], 16)
            for t, v in ((bv_bc, bv), (bo_bc, bo), (g2_bc, ln2_g), (b2ln_bc, ln2_b), (rb_bc, router_b)):
                sp.dma_start(t[:, :], v.rearrange("(o d) -> o d", o=1).to_broadcast([P, v.shape[0]])).then_inc(s["bc_in"], 16)
            sp.dma_start(rw_s[:, :], router_w).then_inc(s["rw_in"], 16)
            sp.wait_ge(s["pool_init"], 1)
            for t in range(TPC):
                sp.dma_start(b2_blk[NE * t:NE * t + NE, t, :], b2).then_inc(s["b2_in"], 16)
            sp.dma_start(w1_s[:, :, :], w1.rearrange("e d f -> d e f")).then_inc(s["w1_in"], 16)
            for e in range(NE):
                sp.dma_start(w2_s[:, e, :, :], w2[e].rearrange("(c f) d -> f c d", f=P)).then_inc(s["w2_in"], 16)
            out_v = out.rearrange("b s d -> s b d")
            with sp.Fori(0, NG) as g:
                sp.wait_ge(s["o_r"], g + 1)
                sp.dma_start(out_v[:, bass.ds(g * TPC, TPC), :], o_s[:, :, :]).then_inc(s["out_done"], 16)
            sp.wait_ge(s["out_done"], 16 * NG)

        @block.gpsimd
        def _(pool):
            pool.memset(ident[:, :], 0.0).then_inc(s["ident_done"], 1)
            pool.memset(ident_bf[:, :], 0.0).then_inc(s["ident_done"], 1)
            pool.wait_ge(s["ident_done"], 2)
            for m in (ident[:, :], ident_bf[:, :]):
                pool.affine_select(out=m, in_=m, compare_op=ALU.not_equal, fill=1.0, base=0,
                                   pattern=[[-1, P]], channel_multiplier=1).then_inc(s["ident_done"], 1)
            pool.memset(b2_blk[:, :, :], 0.0).then_inc(s["pool_init"], 1)
            for d in range(2):
                pool.memset(h[d][:, :], 0.0).then_inc(s["pool_init"], 1)
            pool.memset(a_buf[0][:, :, :, 0:1], 0.0).then_inc(s["pool_init"], 1)
            pool.memset(a_buf[1][:, :, :, P - 1:P], 0.0).then_inc(s["pool_init"], 1)
            for t in range(TPC):
                pool.memset(v_z[:, t, :], 0.0).then_inc(s["pool_init"], 1)
            pool.wait_ge(s["pool_init"], 5 + TPC)
            for t in range(TPC):
                for o in ones_in_v(t):
                    pool.memset(o, 1.0).then_inc(s["pool_init"], 1)

            def decay(l, k, dirs=1):
                n, i = l * STEPS + k, k % 4
                wait(pool, "gated", n + dirs)
                wait(pool, "s_ready", n - 2)
                pool.tensor_tensor(b_buf[:, i, :], z_buf[:, i, :], t_buf[:, i, :],
                                   ALU.mult).then_inc(s["decay"], dirs)
                for d in ((k % 2,) if dirs == 1 else (0, 1)):
                    keep = slice(1, P) if d == 0 else slice(0, P - 1)
                    pool.tensor_scalar(a_buf[d][:, (k // 2) % 2, :, keep], tiles(z_buf[:, i, :])[:, :, keep],
                                       -1.0, 1.0, ALU.mult, ALU.add).then_inc(s["decay"], 1)

            for k in range(0, STEPS, 2):
                decay(0, k, dirs=2)
            with pool.Fori(1, LAYERS) as l:
                for k in range(STEPS):
                    decay(l, k)

            pool.wait_ge(s["bc_in"], 16 * 5)
            pool.wait_ge(s["mask_done"], 1)

            def residual(g):
                pool.wait_ge(s["xn_r"], g + 1)
                wait(pool, "r1_r", g)
                pool.tensor_tensor(xnb[:, :, :], xn[:, :, :], bo_bc[:, :].unsqueeze(1).to_broadcast([P, TPC, P]),
                                   ALU.add).then_inc(s["xnb_r"], 1)

            def query_heads(g):
                pool.wait_ge(s["q_r"], g + 1)
                pool.tensor_tensor(q_m[:, 0, :], q_s[:, :], head_mask[:, 0:1].to_broadcast([P, CHUNK]), ALU.mult)
                for i in range(1, NHEAD):
                    last = pool.tensor_scalar(q_m[:, i, :], q_s[:, :], head_mask[:, i:i + 1], 1.0,
                                              ALU.mult, ALU.mult)
                last.then_inc(s["q_heads_r"], 1)

            def add_expert(g, e):
                pool.wait_ge(s["ym_r"], NE * g + e + 1)
                if e == 1:
                    pool.wait_ge(s["acc0_r"], g + 1)
                else:
                    pool.wait_ge(s["acc_r"], (NE - 1) * g + e - 1)
                pool.tensor_tensor(acc[:, :, :], acc[:, :, :], ym[:, e % 2, :, :],
                                   ALU.add).then_inc(s["acc_r"], 1)

            def finish(g):
                pool.wait_ge(s["x1_r"], g + 1)
                pool.tensor_tensor(x1b[:, :, :], x_rows[:, bass.ds(g * TPC, TPC), :],
                                   b2ln_bc[:, :].unsqueeze(1).to_broadcast([P, TPC, P]),
                                   ALU.add).then_inc(s["fin_pool"], 1)
                pool.wait_ge(s["xh2_r"], g + 1)
                wait(pool, "out_done", 16 * g)
                pool.tensor_tensor(o_s[:, :, :], xh2[:, :, :], g2_bc[:, :].unsqueeze(1).to_broadcast([P, TPC, P]),
                                   ALU.mult).then_inc(s["fin_pool"], 1)
                pool.wait_ge(s["fin_pool"], 2 * g + 2)
                pool.tensor_tensor(o_s[:, :, :], o_s[:, :, :], x1b[:, :, :], ALU.add).then_inc(s["o_r"], 1)

            def group(g, moe=True, more=True):
                residual(g)
                if moe:
                    add_expert(g - 1, 1)
                if more:
                    query_heads(g + 1)
                if moe:
                    add_expert(g - 1, 2)
                    add_expert(g - 1, 3)
                    finish(g - 1)

            query_heads(0)
            group(0, moe=False)
            with pool.Fori(1, NG - 1) as g:
                group(g)
            group(NG - 1, more=False)
            for e in range(1, NE):
                add_expert(NG - 1, e)
            finish(NG - 1)

        @block.tensor
        def _(pe):
            def turn(dst, src, n=P):
                return pe.transpose(dst, src, ident[0:n, 0:n])

            pe.wait_ge(s["ident_done"], 4)
            pe.wait_ge(s["ctx_in"], 16)
            for l in range(LAYERS):
                last = turn(bank[0][:, l * P:(l + 1) * P], ctx_rows[:, l, :])
            last.then_inc(s["prep_T"], 1)
            pe.wait_ge(s["vec_in"], 16 * 9)
            turn(bank[1][:, 0:NVEC], vec_rows[:, :], NVEC).then_inc(s["prep_T"], 1)
            pe.wait_ge(s["fw_in"], 16)
            for a in range(2):
                last = turn(bank[6][:, a * P:(a + 1) * P], fw_rows[:, a, :])
            last.then_inc(s["prep_T"], 1)
            for c in range(NG):
                pe.wait_ge(s["x_norm"], c + 1)
                for t in range(TPC):
                    last = turn(rows_bank(c)[:, t * P:(t + 1) * P], n_buf[:, c, t, :])
                last.then_inc(s["x_rowsT"], 1)

            def gate_in(l, k, layer0=False):
                n = l * STEPS + k
                if layer0:
                    wait(pe, "gated", n - 2)
                    pe.wait_ge(s["x_cols"], k // 2 + 1)
                    pe.matmul(u_bank(k, True)[:, :], gate_wT[:, 0, 0:P], xT[:, chunk_of(k)],
                              start=True, stop=True).then_inc(s["u_ready"], 2)
                    return
                if k == 0:
                    pe.wait_ge(s["w_cur"], l)
                wait(pe, "gated", n - 1)
                wait(pe, "h_ready", n - STEPS + 1)
                pe.matmul(u_bank(k, False)[:, :], gate_cur[:, 0:P], h[k % 2][:, chunk_of(k)],
                          start=True, stop=True).then_inc(s["u_ready"], 1)

            def to_rows(l, k):
                n, m = l * STEPS + k, l * (STEPS // 2) + k // 2
                if isinstance(l, int) and l == 0 and k < 4:
                    pe.wait_ge(s["x_cols"], k + 1)
                wait(pe, "s_ready", n + 1)
                wait(pe, "n_dve" if k % 2 == 0 else "n_act", m - 1)
                src = h[k % 2][:, chunk_of(k)]
                for t in range(TPC):
                    dst = rows_bank(k)[:, t * P:(t + 1) * P]
                    pe.matmul(dst, s_buf[:, k % 4, t * P:(t + 1) * P], ident[:, :], is_transpose=True,
                              start=True, stop=False)
                    last = pe.matmul(dst, src[:, t * P:(t + 1) * P], ident[:, :], is_transpose=True,
                                     start=False, stop=True)
                last.then_inc(s["rows_ready"], 1)

            def to_cols(l, k):
                n, m = l * STEPS + k, l * (STEPS // 2) + k // 2
                wait(pe, "n_dve" if k % 2 == 0 else "n_act", m + 1)
                wait(pe, "h_ready", n - 1)
                for t in range(TPC):
                    last = turn(cols_bank(k)[:, t * P:(t + 1) * P], n_buf[:, k % 4, t, :])
                last.then_inc(s["cols_ready"], 1)

            pe.wait_ge(s["prep_cols"], 3)
            pe.wait_ge(s["pool_init"], 3)
            def window(l, j, first=0, last=PAIRS, gates=True, layer0=False):
                if first <= j - 2 < last:
                    to_rows(l, 2 * j - 3)
                if gates:
                    gate_in(l, 2 * j, layer0)
                    if not layer0:
                        gate_in(l, 2 * j + 1)
                if first <= j - 3 < last:
                    to_cols(l, 2 * j - 6)
                    to_cols(l, 2 * j - 5)
                if first <= j - 1 < last:
                    to_rows(l, 2 * j - 2)

            for j in range(PAIRS):
                window(0, j, layer0=True)
            with pe.Fori(1, LAYERS) as l:
                for j in range(PAIRS):
                    window(l, j, first=-PAIRS)
            for j in range(PAIRS, PAIRS + 3):
                window(LAYERS - 1, j, gates=False)

            def fusion(g):
                pe.matmul(bank[6][:, :], fwT[:, 0, :], h[0][:, bass.ds(g * CHUNK, CHUNK)], start=True, stop=False)
                pe.matmul(bank[6][:, :], fwT[:, 1, :], h[1][:, bass.ds(g * CHUNK, CHUNK)], start=False,
                          stop=True).then_inc(s["fus_p"], 1)

            def turn_fusion(g):
                pe.wait_ge(s["fus_s"], g + 1)
                for t in range(TPC):
                    last = turn(bank[7][:, t * P:(t + 1) * P], fus[:, t * P:(t + 1) * P])
                last.then_inc(s["fusT_p"], 1)

            def turn_xn(g):
                pe.wait_ge(s["xn_r"], g + 1)
                for t in range(TPC):
                    last = turn(bank[6][:, t * P:(t + 1) * P], xn[:, t, :])
                last.then_inc(s["xnT_p"], 1)

            def queries_keys(g):
                pe.wait_ge(s["xnT_s"], g + 1)
                pe.matmul(bank[6][:, :], wq_s[:, :], xnT[:, :], start=True, stop=True).then_inc(s["q_p"], 1)
                pe.wait_ge(s["x1_r"], g + 1)
                pe.matmul(bank[7][:, :], wk_s[:, :], xnT[:, :], start=True, stop=True).then_inc(s["k_p"], 1)

            def values(g):
                pe.wait_ge(s["k_r"], g + 1)
                for t in range(TPC):
                    last = pe.matmul(bank[7][:, t * P:(t + 1) * P], xnT[:, t * P:(t + 1) * P], wv_s[:, :],
                                     start=True, stop=True)
                last.then_inc(s["v_p"], 1)

            def score_for_max(g, t, j):
                if t == 0 and j == 0:
                    pe.wait_ge(s["qbf_r"], g + 1)
                    pe.wait_ge(s["k_heads_r"], g + 1)
                wait(pe, "mx_r", NHEAD * g + 4 * t + j - 1)
                q_t, k_t = q_bf[:, t * P:(t + 1) * P], k_m[:, 4 * j:4 * j + 4, t * P:(t + 1) * P]
                pe.matmul(bank[j % 2][:, :], q_t, k_t, start=True, stop=True).then_inc(s["sc_p"], 1)

            def shifted_scores(g, t):
                if t == 0:
                    pe.wait_ge(s["q_heads_r"], g + 1)
                pe.wait_ge(s["mneg_r"], TPC * g + t + 1)
                for j in range(4):
                    wait(pe, "exp_r", NHEAD * g + 4 * t + j - 1)
                    dst = bank[2 + j % 2]
                    k_t, q_t = k_s[:, t * P:(t + 1) * P], q_m[:, 4 * j:4 * j + 4, t * P:(t + 1) * P]
                    pe.matmul(dst[:, :], k_t, q_t, start=True, stop=False, skip_group_check=True)
                    for i4 in range(4):
                        hh = 4 * j + i4
                        last = pe.matmul(dst[:, i4 * P:(i4 + 1) * P],
                                         mneg[:, t % 2, hh:hh + 1].to_broadcast([P, P]), ident_bf[:, :],
                                         start=False, stop=(i4 == 3), skip_group_check=True)
                    last.then_inc(s["st_p"], 1)
                    if t < TPC - 1:
                        score_for_max(g, t + 1, j)

            def weighted_values(g, t, moe):
                pe.wait_ge(s["exp_r"], NHEAD * g + 4 * t + 4)
                if t == 0:
                    pe.wait_ge(s["v_r"], g + 1)
                    if moe:
                        pe.wait_ge(s["acc0_r"], g)
                else:
                    pe.wait_ge(s["att_r"], TPC * g + t)
                for half in range(2):
                    for i in range(8):
                        hh = 8 * half + i
                        last = pe.matmul(bank[4][:, half * P:(half + 1) * P], v_z[:, t, hh * P:(hh + 1) * P],
                                         probs[:, t % 2, hh, :], start=(i == 0), stop=(i == 7))
                last.then_inc(s["pv_p"], 1)

            def project(g):
                pe.wait_ge(s["att_r"], TPC * (g + 1))
                for t in range(TPC):
                    last = pe.matmul(bank[4][:, t * P:(t + 1) * P], att[:, t * P:(t + 1) * P], wo_s[:, :],
                                     start=True, stop=True)
                last.then_inc(s["wo_p"], 1)

            def back_to_cols(g, moe):
                pe.wait_ge(s["xh1_r"], g + 1)
                if moe:
                    pe.wait_ge(s["relu_r"], NE * FC * g)
                for t in range(TPC):
                    last = turn(bank[6][:, t * P:(t + 1) * P], xh[:, t, :])
                last.then_inc(s["xh1T_p"], 1)

            def router(g):
                pe.wait_ge(s["xaT_s"], g + 1)
                for t in range(TPC):
                    pe.matmul(bank[4][:, t * P:(t + 1) * P], xaT[:, t * P:(t + 1) * P], ident[:, :],
                              start=(t == 0), stop=False, skip_group_check=True)
                wait(pe, "ym_r", NE * g)
                for t in range(TPC):
                    last = pe.matmul(bank[5][:, t:t + 1], xaT[:, t * P:(t + 1) * P], rw_s[:, :],
                                     start=True, stop=True)
                last.then_inc(s["key_p"], 1)

            def turn_mask(g):
                pe.wait_ge(s["mask_r"], g + 1)
                turn(bank[5][0:TPC * NE, 0:P], mask[:, :, :].rearrange("p t e -> p (t e)")).then_inc(s["maskT_p"], 1)

            def routed_bias(g):
                pe.wait_ge(s["maskT_s"], g + 1)
                pe.matmul(bank[4][:, :], maskT[:, :], b2_blk[:, :, :],
                          start=False, stop=True, skip_group_check=True).then_inc(s["b2_p"], 1)

            def hidden(g, e, behind=(), flip=0, pieces=range(FC)):
                for c in pieces:
                    if c < 2 and behind:
                        name, value = behind[c]
                        pe.wait_ge(s[name], value)
                    wait(pe, "relu_r", NE * FC * g + FC * e + c - 1)
                    pe.matmul(bank[6 + (c + flip) % 2][:, :], w1_s[:, e, c * P:(c + 1) * P], xaT[:, :],
                              start=True, stop=True).then_inc(s["hid_p"], 1)

            def expert_out(g, e, t):
                if t == 0:
                    pe.wait_ge(s["relu_r"], NE * FC * g + FC * (e + 1))
                    if e:
                        pe.wait_ge(s["ym_r"], NE * g + e)
                for c in range(FC):
                    last = pe.matmul(bank[5][:, t * P:(t + 1) * P], hid[:, e % 2, c, t * P:(t + 1) * P],
                                     w2_s[:, e, c, :], start=(c == 0), stop=(c == FC - 1))
                if t == TPC - 1:
                    last.then_inc(s["y_p"], 1)

            def expert(g, e):
                for t in range(TPC):
                    expert_out(g, e, t)

            def group(g, moe=True, more=True):
                m = g - 1
                shifted_scores(g, 0)
                if more:
                    fusion(g + 1)
                if moe:
                    hidden(m, 1, (("v_r", g + 1), ("fus_s", g + 2)) if more else (), flip=more)
                shifted_scores(g, 1)
                weighted_values(g, 0, moe)
                if more:
                    if moe:
                        pe.wait_ge(s["relu_r"], NE * FC * m + 2 * FC)
                    turn_fusion(g + 1)
                if moe:
                    expert(m, 1)
                shifted_scores(g, 2)
                weighted_values(g, 1, moe)
                if more:
                    turn_xn(g + 1)
                if moe:
                    hidden(m, 2, (("x1_r", g + 2), ("xnT_s", g + 2)) if more else (), flip=more)
                shifted_scores(g, 3)
                weighted_values(g, 2, moe)
                if more:
                    if moe:
                        pe.wait_ge(s["relu_r"], NE * FC * m + 3 * FC)
                    queries_keys(g + 1)
                weighted_values(g, 3, moe)
                if moe:
                    hidden(m, 3, (("q_r", g + 2), ("k_r", g + 2)) if more else (), pieces=range(2))
                project(g)
                if moe:
                    hidden(m, 3, pieces=range(2, FC))
                if moe:
                    expert(m, 2)
                if more:
                    if moe:
                        pe.wait_ge(s["relu_r"], NE * FC * g)
                    values(g + 1)
                back_to_cols(g, moe)
                if moe:
                    expert(m, 3)
                router(g)
                hidden(g, 0, (("xaT_s", g + 1), ("v_r", g + 2)) if more else (), pieces=range(3))
                if more:
                    score_for_max(g + 1, 0, 0)
                turn_mask(g)
                hidden(g, 0, pieces=(3,))
                if more:
                    score_for_max(g + 1, 0, 1)
                routed_bias(g)
                if not more:
                    hidden(g, 1)
                expert_out(g, 0, 0)
                if more:
                    score_for_max(g + 1, 0, 2)
                expert_out(g, 0, 1)
                if more:
                    score_for_max(g + 1, 0, 3)
                expert_out(g, 0, 2)
                expert_out(g, 0, 3)

            pe.wait_ge(s["h_ready"], LAYERS * STEPS)
            fusion(0)
            turn_fusion(0)
            turn_xn(0)
            pe.wait_ge(s["attw_in"], 64)
            queries_keys(0)
            values(0)
            for j in range(4):
                score_for_max(0, 0, j)
            for name, v in (("w1_in", 16), ("w2_in", 64), ("b2_in", 64), ("rw_in", 16), ("pool_init", 5 + 3 * TPC)):
                pe.wait_ge(s[name], v)
            group(0, moe=False)
            with pe.Fori(1, NG - 1) as g:
                group(g)
            group(NG - 1, more=False)
            hidden(NG - 1, 2)
            expert(NG - 1, 1)
            hidden(NG - 1, 3)
            expert(NG - 1, 2)
            expert(NG - 1, 3)

        @block.scalar
        def _(act):
            act.wait_ge(s["prep_T"], 1)
            act.activation(gate_wT[:, :, 0:P], tiles(bank[0][:, :]), ACT.Identity).then_inc(s["prep_cols"], 1)
            act.wait_ge(s["prep_T"], 2)
            act.activation(vec[:, :], bank[1][:, 0:NVEC], ACT.Identity)
            act.activation(gate_wT[:, :, P], bank[1][:, R_COND:R_COND + LAYERS], ACT.Identity).then_inc(s["prep_cols"], 1)
            act.wait_ge(s["prep_T"], 3)
            act.activation(fwT[:, :, :], bank[6][:, 0:2 * P].rearrange("p (a h) -> p a h", a=2),
                           ACT.Identity).then_inc(s["prep_cols"], 1)
            for c in range(NG):
                act.wait_ge(s["x_rowsT"], c + 1)
                act.activation(xT[:, c * CHUNK:(c + 1) * CHUNK], rows_bank(c)[:, :], ACT.Identity).then_inc(s["x_cols"], 1)
            act.wait_ge(s["prep_cols"], 3)

            def gates(l, k, layer0=False):
                n, i = l * STEPS + k, k % 4
                dirs = 2 if layer0 else 1
                wait(act, "u_ready", n + dirs)
                wait(act, "decay", 2 * (n - 2))
                src = u_bank(k, layer0)[:, :]
                bias = gate_wT[:, 0, P:P + 1] if layer0 else gate_cur[:, P:P + 1]
                act.activation(z_buf[:, i, :], src, ACT.Sigmoid, bias=bias)
                act.activation(t_buf[:, i, :], src, ACT.Tanh, bias=bias).then_inc(s["gated"], dirs)

            def norm(l, k):
                n, m = l * STEPS + k, l * (STEPS // 2) + k // 2
                slot = (k // 2) % 2
                wait(act, "coef", m + 1)
                wait(act, "cols_ready", n - 3)
                for t in range(TPC):
                    last = act.activation(n_buf[:, k % 4, t, :], rows_bank(k)[:, t * P:(t + 1) * P], ACT.Identity,
                                          scale=co[:, slot, 0, TPC + t:TPC + t + 1],
                                          bias=co[:, slot, 1, TPC + t:TPC + t + 1])
                last.then_inc(s["n_act"], 1)

            def affine(l, k):
                wait(act, "cols_ready", l * STEPS + k + 1)
                act.activation(h[k % 2][:, chunk_of(k)], cols_bank(k)[:, :], ACT.Identity,
                               scale=col(R_GAMMA), bias=col(R_BETA)).then_inc(s["h_ready"], 1)

            def window(l, j, first=0, last=PAIRS, gated=True, layer0=False):
                if gated:
                    gates(l, 2 * j, layer0)
                if first <= j - 3 < last:
                    norm(l, 2 * j - 5)
                if gated and not layer0:
                    gates(l, 2 * j + 1)
                if first <= j - 3 < last:
                    affine(l, 2 * j - 6)
                    affine(l, 2 * j - 5)

            for j in range(PAIRS):
                window(0, j, layer0=True)
            with act.Fori(1, LAYERS) as l:
                act.wait_ge(s["u_ready"], l * STEPS)
                act.wait_ge(s["gated"], l * STEPS)
                act.activation(gate_cur[:, :], gate_wT[:, bass.ds(l, 1), :].rearrange("p o c -> p (o c)"),
                               ACT.Identity).then_inc(s["w_cur"], 1)
                act.wait_ge(s["w_cur"], l)
                for j in range(PAIRS):
                    window(l, j, first=-PAIRS)
            for j in range(PAIRS, PAIRS + 3):
                window(LAYERS - 1, j, gated=False)

            def fusion(g):
                act.wait_ge(s["fus_p"], g + 1)
                act.activation(fus[:, :], bank[6][:, :], ACT.Identity, bias=col(R_FB)).then_inc(s["fus_s"], 1)

            def xn_cols(g):
                act.wait_ge(s["xnT_p"], g + 1)
                act.activation(xnT[:, :], bank[6][:, :], ACT.Identity).then_inc(s["xnT_s"], 1)

            def queries_keys(g):
                act.wait_ge(s["q_p"], g + 1)
                wait(act, "q_heads_r", g)
                act.activation(q_s[:, :], bank[6][:, :], ACT.Identity, bias=col(R_BQ)).then_inc(s["q_r"], 1)
                act.wait_ge(s["k_p"], g + 1)
                act.activation(k_s[:, :], bank[7][:, :], ACT.Identity, bias=col(R_BK)).then_inc(s["k_r"], 1)
                act.wait_ge(s["k_r"], g + 1)
                wait(act, "k_heads_r", g)
                act.activation(k_bf[:, :], k_s[:, :], ACT.Identity).then_inc(s["kbf_r"], 1)
                act.activation(q_bf[:, :], q_s[:, :], ACT.Identity).then_inc(s["qbf_r"], 1)

            def exps(g, t):
                wait(act, "pv_p", TPC * g + t - 1)
                for j in range(4):
                    act.wait_ge(s["st_p"], NHEAD * g + 4 * t + j + 1)
                    act.activation(probs[:, t % 2, 4 * j:4 * j + 4, :], tiles(bank[2 + j % 2][:, :]), ACT.Exp,
                                   scale=SCALE).then_inc(s["exp_r"], 1)

            def prob_sums(g, t):
                act.wait_ge(s["pv_p"], TPC * g + t + 1)
                act.activation(sums[64:128, t % 2, :], bank[4][64:128, 0:P], ACT.Identity)
                act.activation(sums[0:64, t % 2, :], bank[4][0:64, P:2 * P], ACT.Identity).then_inc(s["sums_r"], 1)

            def xa_cols(g):
                act.wait_ge(s["xh1T_p"], g + 1)
                act.activation(xaT[:, :], bank[6][:, :], ACT.Identity, scale=col(R_G1),
                               bias=col(R_B1LN)).then_inc(s["xaT_s"], 1)

            def relu(g, e, flip=0, pieces=range(FC)):
                for c in pieces:
                    act.wait_ge(s["hid_p"], NE * FC * g + FC * e + c + 1)
                    act.activation(hid[:, e % 2, c, :], bank[6 + (c + flip) % 2][:, :], ACT.Relu,
                                   bias=col(R_B1 + FC * e + c)).then_inc(s["relu_r"], 1)

            def mask_rows(g):
                act.wait_ge(s["maskT_p"], g + 1)
                act.activation(maskT[:, :], bank[5][0:TPC * NE, 0:P], ACT.Identity).then_inc(s["maskT_s"], 1)

            def group(g, moe=True, more=True):
                m = g - 1
                exps(g, 0)
                if more:
                    fusion(g + 1)
                if moe:
                    relu(m, 1, flip=more)
                exps(g, 1)
                prob_sums(g, 0)
                exps(g, 2)
                prob_sums(g, 1)
                if more:
                    xn_cols(g + 1)
                if moe:
                    relu(m, 2, flip=more)
                exps(g, 3)
                prob_sums(g, 2)
                if more:
                    queries_keys(g + 1)
                prob_sums(g, 3)
                if moe:
                    relu(m, 3)
                xa_cols(g)
                relu(g, 0, pieces=range(3))
                mask_rows(g)
                relu(g, 0, pieces=(3,))

            fusion(0)
            xn_cols(0)
            queries_keys(0)
            group(0, moe=False)
            with act.Fori(1, NG - 1) as g:
                group(g)
            group(NG - 1, more=False)
            for e in range(1, NE):
                relu(NG - 1, e)

        @block.vector
        def _(dve):
            ch = Chain(dve, s["dve1"])
            for c in range(NG):
                dve.wait_ge(x_in[c], 16)
                token_stats(dve, ch, lambda i: x_rows[:, TPC * c + i, :], c % 2)
                ch.then(Coefficients(dve, ch, c % 2, TPC).finish())
                normalise(dve, lambda i: n_buf[:, c, i, :], lambda i: x_rows[:, TPC * c + i, :],
                          c % 2).then_inc(s["x_norm"], 1)
            dve.wait_ge(s["ident_done"], 4)
            dve.reduce_sum(head_mask[:, :], ident[:, :].rearrange("p (h y) -> p h y", y=HD),
                           AX.X).then_inc(s["mask_done"], 1)
            dve.wait_ge(s["mask_done"], 1)
            dve.wait_ge(s["pool_init"], 5)

            def clip(ch, l, k, layer0=False):
                n, d = l * STEPS + k, k % 2
                a = a_buf[d][:, (k // 2) % 2, :, slice(1, P) if d == 0 else slice(0, P - 1)]
                wait(dve, "decay", 2 * (n + (2 if layer0 and d == 0 else 1)))
                ch.mark(dve.tensor_scalar(a, a, CLAMP_LO, CLAMP_HI, ALU.max, ALU.min))
                return ch.n

            def scan(ch, l, k, clipped, layer0=False):
                n, d, i = l * STEPS + k, k % 2, ((k - k % 2) if layer0 else k) % 4
                dve.wait_ge(ch.sm, ch.base + clipped)
                wait(dve, "rows_ready", n - 3)
                a = a_buf[d][:, (k // 2) % 2, :, :].rearrange("p t c -> p (t c)")
                b, out_s = b_buf[:, i, :], s_buf[:, k % 4, :]
                if d:
                    a, b, out_s = a[:, ::-1], b[:, ::-1], out_s[:, ::-1]
                dve.tensor_tensor_scan(out_s, a, b, 0.0, ALU.mult, ALU.add).then_inc(s["s_ready"], 1)

            def stats(ch, l, k, between):
                wait(dve, "rows_ready", l * STEPS + k + 1)
                token_stats(dve, ch, lambda i: rows_bank(k)[:, i * P:(i + 1) * P], (k // 2) % 2, TPC * (k % 2),
                            between)

            def norm(l, k, between):
                wait(dve, "coef", l * PAIRS + k // 2 + 1)
                wait(dve, "cols_ready", l * STEPS + k - 3)
                normalise(dve, lambda i: n_buf[:, k % 4, i, :], lambda i: rows_bank(k)[:, i * P:(i + 1) * P],
                          (k // 2) % 2, between=between).then_inc(s["n_dve"], 1)

            SPLIT = 7

            def window(ch, l, j, first=0, last=PAIRS, scans=True, layer0=False):
                old = new = None
                if first <= j - 2 < last:
                    wait(dve, "n_act", l * PAIRS + j - 3)
                    old = Coefficients(dve, ch, j % 2, 2 * TPC, at=SPLIT)

                def old_link():
                    if old and old.i < old.LINKS:
                        final = old.next()
                        if final:
                            final.then_inc(s["coef"], 1)

                def new_link():
                    if new and new.i < SPLIT:
                        new.next()

                if first <= j - 1 < last:
                    for k in (2 * j - 2, 2 * j - 1):
                        stats(ch, l, k, between=old_link)
                    new = Coefficients(dve, ch, (j - 1) % 2, 2 * TPC)
                while old and old.i < old.LINKS:
                    old_link()
                if old:
                    norm(l, 2 * j - 4, between=new_link)
                if scans:
                    for k in (2 * j, 2 * j + 1):
                        clipped = clip(ch, l, k, layer0)
                        new_link()
                        scan(ch, l, k, clipped, layer0)
                        new_link()
                while new and new.i < SPLIT:
                    new_link()

            for j in range(PAIRS):
                window(ch, 0, j, layer0=True)
            PER_LAYER = 2 * STEPS + PAIRS * (Coefficients.LINKS - 1)
            before = ch.n
            with dve.Fori(1, LAYERS) as l:
                ch = Chain(dve, s["dve1"], (l - 1) * PER_LAYER + before)
                for j in range(PAIRS):
                    window(ch, l, j, first=-PAIRS)
                assert ch.n == PER_LAYER
            ch = Chain(dve, s["dve1"], before + (LAYERS - 1) * PER_LAYER)
            for j in range(PAIRS, PAIRS + 2):
                window(ch, LAYERS - 1, j, scans=False)

            class Norm:

                LINKS = Coefficients.LINKS

                def __init__(self, ch, src):
                    self.src = src
                    token_stats(dve, ch, src, 0)
                    self.co = Coefficients(dve, ch, 0, TPC)

                def link(self, n=1):
                    if self.co.i + n < self.co.LINKS:
                        self.co.next(n)

                def finish(self, ch, dst, name):
                    ch.then(self.co.finish())
                    normalise(dve, dst, self.src, 0).then_inc(s[name], 1)

            def no_link():
                pass

            def front_rows(ch, g):
                dve.wait_ge(s["fusT_p"], g + 1)
                x_g = x_rows[:, bass.ds(g * TPC, TPC), :]
                ch.then(dve.tensor_tensor(x1[:, :, :], tiles(bank[7][:, :]), x_g, ALU.add))
                norm = Norm(ch, lambda i: x1[:, i, :])
                dve.tensor_copy(x_g, x1[:, :, :]).then_inc(s["x1_r"], 1)
                return norm

            def finish_front(ch, g, norm):
                wait(dve, "xnb_r", g)
                norm.finish(ch, lambda i: xn[:, i, :], "xn_r")

            def value_rows(g):
                dve.wait_ge(s["v_p"], g + 1)
                for half, dst in enumerate(v_dims):
                    at = slice(64 * half, 64 * half + 64)
                    src = tiles(bank[7][:, :])[:, :, at].rearrange("p t (h y) -> p t h y", y=HD)
                    bias = bv_bc[:, at].rearrange("p (h y) -> p h y", y=HD).unsqueeze(1).to_broadcast([P, TPC, 8, HD])
                    last = dve.tensor_tensor(dst, src, bias, ALU.add)
                last.then_inc(s["v_r"], 1)

            def key_heads(g, first, last):
                if first == 0:
                    dve.wait_ge(s["kbf_r"], g + 1)
                for i in range(first, last):
                    ins = dve.tensor_scalar(k_m[:, i, :], k_bf[:, :], head_mask[:, i:i + 1], None, ALU.mult)
                if last == NHEAD:
                    ins.then_inc(s["k_heads_r"], 1)

            def maxima(g, t, between=no_link):
                for j in range(4):
                    dve.wait_ge(s["sc_p"], NHEAD * g + 4 * t + j + 1)
                    dve.reduce_max(mx[:, t % 2, 4 * j:4 * j + 4], tiles(bank[j % 2][:, :]),
                                   AX.X).then_inc(s["mx_r"], 1)
                    between()
                dve.wait_ge(s["mx_r"], NHEAD * g + 4 * t + 4)
                wait(dve, "st_p", NHEAD * g + 4 * t - 4)
                dve.tensor_scalar(mneg[:, t % 2, :], mx[:, t % 2, :], -1.0, None, ALU.mult).then_inc(s["mneg_r"], 1)

            def attended(ch, g, t, between=no_link):
                dve.wait_ge(s["sums_r"], TPC * g + t + 1)
                if t == 0:
                    wait(dve, "wo_p", g)
                ch.mark(dve.reciprocal(rsums[:, t % 2, :], sums[:, t % 2, :]))
                between()
                dve.wait_ge(ch.sm, ch.base + ch.n)
                at = slice(t * P, (t + 1) * P)
                dve.tensor_tensor(att[0:64, at], bank[4][0:64, 0:P], rsums[64:128, t % 2, :], ALU.mult)
                dve.tensor_tensor(att[64:128, at], bank[4][64:128, P:2 * P], rsums[0:64, t % 2, :],
                                  ALU.mult).then_inc(s["att_r"], 1)

            def first_norm(ch, g):
                dve.wait_ge(s["wo_p"], g + 1)
                dve.wait_ge(s["xnb_r"], g + 1)
                dve.tensor_tensor(r1[:, :, :], tiles(bank[4][:, :]), xnb[:, :, :], ALU.add).then_inc(s["r1_r"], 1)
                dve.wait_ge(s["r1_r"], g + 1)
                return Norm(ch, lambda i: r1[:, i, :])

            def floor(ch, dst, src, flag):
                ch.then(dve.tensor_copy(ki[:, :], src))
                ch.then(dve.tensor_copy(dst, ki[:, :]))
                ch.then(dve.tensor_tensor(flag, dst, src, ALU.is_gt))
                ch.then(dve.tensor_tensor(dst, dst, flag, ALU.subtract))

            def route(ch, g):
                dve.wait_ge(s["key_p"], g + 1)
                ch.then(dve.tensor_scalar(key[:, :], bank[5][:, 0:TPC], rb_bc[:, :], None, ALU.add))
                fl, quarter, fq, flag = (kf[:, i, :] for i in range(4))
                floor(ch, fl, key[:, :], flag)
                ch.then(dve.tensor_scalar(quarter, fl, 1.0 / NE, None, ALU.mult))
                floor(ch, fq, quarter, flag)
                ch.then(dve.scalar_tensor_tensor(out=fl, in0=fq, scalar=-float(NE), in1=fl, op0=ALU.mult, op1=ALU.add))
                wait(dve, "maskT_p", g)
                for e in range(NE):
                    last = dve.tensor_scalar(mask[:, :, e], fl, float(e), None, ALU.is_equal)
                last.then_inc(s["mask_r"], 1)

            def masked(g, e):
                dve.wait_ge(s["y_p"], NE * g + e + 1)
                if e == 3:
                    dve.wait_ge(s["acc_r"], 3 * g + 1)
                dve.tensor_tensor(ym[:, e % 2, :, :], tiles(bank[5][:, :]),
                                  mask[:, :, e:e + 1].to_broadcast([P, TPC, P]), ALU.mult).then_inc(s["ym_r"], 1)

            def first_expert(g):
                dve.wait_ge(s["b2_p"], g + 1)
                dve.wait_ge(s["ym_r"], NE * g + 1)
                dve.tensor_tensor(acc[:, :, :], ym[:, 0, :, :], tiles(bank[4][:, :]), ALU.add).then_inc(s["acc0_r"], 1)

            def second_norm(ch, g):
                dve.wait_ge(s["acc_r"], 3 * g + 3)
                return Norm(ch, lambda i: acc[:, i, :])

            def finish_second(ch, g, norm):
                wait(dve, "o_r", g)
                norm.finish(ch, lambda i: xh2[:, i, :], "xh2_r")

            def group(ch, g, moe=True, more=True):
                m = g - 1
                maxima(g, 1)
                if moe:
                    first_expert(m)
                maxima(g, 2)
                norm = front_rows(ch, g + 1) if more else None
                link = norm.link if more else no_link
                attended(ch, g, 0, between=link)
                link()
                if moe:
                    masked(m, 1)
                    link()
                maxima(g, 3, between=link)
                if more:
                    finish_front(ch, g + 1, norm)
                attended(ch, g, 1)
                attended(ch, g, 2)
                attended(ch, g, 3)
                norm = first_norm(ch, g)
                for i in range(norm.LINKS - 1):
                    norm.link()
                    if more:
                        key_heads(g + 1, i, i + 1)
                wait(dve, "xh1T_p", g)
                norm.finish(ch, lambda i: xh[:, i, :], "xh1_r")
                if moe:
                    masked(m, 2)
                if more:
                    value_rows(g + 1)
                    key_heads(g + 1, norm.LINKS - 1, NHEAD)
                if moe:
                    masked(m, 3)
                route(ch, g)
                norm = second_norm(ch, m) if moe else None
                if more:
                    maxima(g + 1, 0, between=norm.link if moe else no_link)
                if moe:
                    finish_second(ch, m, norm)
                masked(g, 0)

            ch = Chain(dve, s["dve2"])
            finish_front(ch, 0, front_rows(ch, 0))
            dve.wait_ge(s["pool_init"], 5 + 3 * TPC)
            dve.wait_ge(s["bc_in"], 16 * 5)
            key_heads(0, 0, NHEAD)
            value_rows(0)
            maxima(0, 0)
            group(ch, 0, moe=False)
            before, PER_GROUP = ch.n, 3 * (Norm.LINKS + 1) + 1 + TPC + 11
            with dve.Fori(1, NG - 1) as g:
                ch = Chain(dve, s["dve2"], (g - 1) * PER_GROUP + before)
                group(ch, g)
                assert ch.n == PER_GROUP, ch.n
            ch = Chain(dve, s["dve2"], before + (NG - 2) * PER_GROUP)
            group(ch, NG - 1, more=False)
            first_expert(NG - 1)
            for e in range(1, NE):
                masked(NG - 1, e)
            finish_second(ch, NG - 1, second_norm(ch, NG - 1))


_P = "L0_ffn_"
_INS = ["x", "ctx_1024", "cond_1024", "L0_xcond_fusion_W", "L0_xcond_fusion_b", "L0_xcond_ln_gamma",
        "L0_xcond_ln_beta"] + [_P + n for n in (
            "Wq", "bq", "Wk", "bk", "Wv", "bv", "Wo", "bo", "router_w", "router_b", "W1", "b1", "W2", "b2",
            "ln1_g", "ln1_b", "ln2_g", "ln2_b")]


def kernel(**inputs):
    import numpy as _np
    import concourse.bacc as _bacc
    from concourse import mybir as _mybir
    from concourse.bass_utils import run_bass_kernel_spmd as _run

    nc = _bacc.Bacc("TRN2", target_bir_lowering=False, num_devices=1)
    arrays, args = {}, []
    for name in _INS:
        a = _np.ascontiguousarray(inputs[name])
        arrays[f"in_{name}_dram"] = a
        args.append(nc.dram_tensor(f"in_{name}_dram", a.shape, _mybir.dt.from_np(a.dtype), kind="ExternalInput").ap())
    shape = _np.shape(inputs["x"])
    args.append(nc.dram_tensor("out_dram", shape, _mybir.dt.float32, kind="ExternalOutput").ap())
    build(nc, *args)
    r = _run(nc, [arrays], core_ids=[0])
    return r.results[0]["out_dram"]
```

```python
from contextlib import ExitStack

import concourse.bass as bass
from concourse import mybir

F32 = mybir.dt.float32
BF16 = mybir.dt.bfloat16
F32R = mybir.dt.float32r
I32 = mybir.dt.int32
U32 = mybir.dt.uint32
ALU = mybir.AluOpType
ACT = mybir.ActivationFunctionType
AX = mybir.AxisListType

P = 128
CHUNK = 512
TPC = CHUNK // P
LAYERS = 4
NHEAD = 16
HD = P // NHEAD
NE = 4
DFF = 512
FC = DFF // P
EPS = 1e-5
CLAMP_LO, CLAMP_HI = 1e-8, 1.0 - 1e-8
RSQRT_MAGIC = float(0x5F1FFF77)
RSQRT_STEPS = ((0.7038757896311395, 1.6818510386049268), (0.50000015752812, 1.5000004725843))
VPITCH = 2048 + 128

R_COND, R_GAMMA, R_BETA, R_FB, R_BQ, R_BK, R_G1, R_B1LN, R_B1 = 0, 4, 5, 6, 7, 8, 9, 10, 11
NVEC = R_B1 + NE * FC

STEPS = 8
QUADS_ACT, QUADS_DVE = ((0, 2), (0, 2, 3)), ((1, 3), (1,))
PAIRS = STEPS // 2


def build(nc, x, ctx_w, cond, fusion_w, fusion_b, ln_gamma, ln_beta, wq, bq, wk, bk, wv, bv, wo, bo,
          router_w, router_b, w1, b1, w2, b2, ln1_g, ln1_b, ln2_g, ln2_b, out):
    B, S, D = x.shape
    NT = B
    NG = NT // TPC
    assert (S, D) == (P, P) and NT % TPC == 0
    SCALE = float(HD) ** -0.5

    with ExitStack() as stack:
        def sb(name, shape, dt=F32):
            return stack.enter_context(nc.sbuf_tensor(name, shape, dt))

        def sem(name):
            return stack.enter_context(nc.semaphore(name))

        bank = [stack.enter_context(nc.psum_tensor(f"bank{i}", [P, 512], F32)) for i in range(8)]

        x_rows = sb("x_rows", [P, NT, P])
        ident = sb("ident", [P, P])
        rw_s = sb("rw_s", [P, 1])
        ident_bf = sb("ident_bf", [P, P], BF16)
        head_mask = sb("head_mask", [P, NHEAD])
        quad_mask = sb("quad_mask", [P, 4])
        sel_k = sb("sel_k", [P, 4, 6, 32], F32R)
        sel_q = sb("sel_q", [P, 4, 5, 32], F32R)
        ctx_rows = sb("ctx_rows", [P, LAYERS, P])
        gate_wT = sb("gate_wT", [P, LAYERS, P + 1])
        gate_cur = sb("gate_cur", [P, P + 1])
        fw_rows = sb("fw_rows", [P, 2, P])
        fwT = sb("fwT", [P, 2, P])
        vec_rows = sb("vec_rows", [NVEC, P])
        vec = sb("vec", [P, NVEC])
        wq_s, wk_s, wv_s, wo_s = (sb(n, [P, P]) for n in ("wq_s", "wk_s", "wv_s", "wo_s"))
        w1_hi, w1_lo = (sb(n, [P, NE, DFF], F32R) for n in ("w1_hi", "w1_lo"))
        w2_s = sb("w2_s", [P, NE, FC, P])
        rb_bc = sb("rb_bc", [P, 1])
        bv_bc, bo_bc, g2_bc, b2ln_bc = (sb(n, [P, P]) for n in ("bv_bc", "bo_bc", "g2_bc", "b2ln_bc"))
        b2_blk = sb("b2_blk", [TPC * NE, TPC, P])
        h = [sb("h_fwd", [P, NT * P]), sb("h_bwd", [P, NT * P])]
        z_and_t = sb("z_and_t", [P, 2, 4, CHUNK])
        z_buf, t_buf = z_and_t[:, 0], z_and_t[:, 1]
        a_buf = [sb("a_fwd", [P, 2, TPC, P]), sb("a_bwd", [P, 2, TPC, P])]
        with nc.sbuf_tensor("work", [P, NHEAD, CHUNK], F32) as work:
            pass
        q_m = sb("q_m", [P, NHEAD, CHUNK], F32R)
        b_buf, s_buf = work[:, 0:4, :], work[:, 4:8, :]
        n_buf = work[:, 8:12, :].rearrange("p k (t c) -> p k t c", c=P)
        xT = work[:, 12:16, :].rearrange("p k c -> p (k c)")
        st = sb("st", [P, 3, 8, 6])
        co = sb("co", [P, 3, 2, 8])
        tmp = sb("tmp", [P, 2, 6, 8])
        fus = sb("fus", [P, CHUNK])
        x1 = fus[:, :].rearrange("p (t c) -> p t c", c=P)
        xn = sb("xn", [P, TPC, P])
        xnb = sb("xnb", [P, TPC, P])
        xnT = sb("xnT", [P, CHUNK])
        q_hi, q_lo, k_hi, k_lo = (sb(n, [P, CHUNK], F32R) for n in ("q_hi", "q_lo", "k_hi", "k_lo"))
        k_st = sb("k_st", [P, NHEAD // 4, CHUNK], F32R)
        v_z = sb("v_z", [P, TPC, VPITCH])
        def v_blocks(off):
            return v_z[:, :, off:off + 8 * 136].rearrange("p t (h y) -> p t h y", y=136)[:, :, :, 0:HD]

        v_dims = (v_blocks(0), v_blocks(1024 + 64))

        def ones_in_v(t):
            return v_blocks(64)[:, t], v_blocks(1024)[:, t]

        mx = sb("mx", [P, 2, NHEAD])
        mneg = sb("mneg", [P, 2, NHEAD], BF16)
        ones_bf = sb("ones_bf", [P, P], BF16)
        probs = sb("probs", [P, 2, NHEAD, P])
        diag = [h[d][:, 0:CHUNK].bitcast(BF16).rearrange("p (i q) -> p i q", q=P) for d in range(2)]

        def diag_of(j):
            return diag[j // 2][:, 4 * (j % 2):4 * (j % 2) + 4, :]

        w1_in = probs[:, 0, :, :].rearrange("p (e a) q -> p e (a q)", e=NE)
        sums = sb("sums", [P, P])
        att = sb("att", [P, CHUNK])
        r1 = gate_wT[:, :, 0:P]
        xh = sb("xh", [P, TPC, P])
        xh2 = xh
        xaT = xnT
        xa_hi, xa_lo = (sb(n, [P, CHUNK], F32R) for n in ("xa_hi", "xa_lo"))
        key = sb("key", [P, TPC])
        kf = sb("kf", [P, 4, TPC])
        ki = sb("ki", [P, TPC], I32)
        mask = sb("mask", [P, TPC, NE])
        maskT = fw_rows[0:TPC * NE, 0, :]
        hid = z_and_t
        ym = a_buf[0]
        acc, x1b = a_buf[1][:, 0], a_buf[1][:, 1]
        o_s = ctx_rows

        names = """x_in0 x_in1 x_in2 x_in3 ctx_in vec_in fw_in rw_in attw_in bc_in b2_in w1_in w1_split w2_in out_done
        ident_done ones_done pool_init mask_done x_norm x_rowsT x_cols prep_T prep_cols
        w_cur u_ready gated decay s_ready rows_ready coef n_dve n_act cols_ready h_ready dve1
        fus_p fus_s fusT_p x1_r xn_r xnT_p xnT_s q_p q_hi_r q_lo_r k_p k_hi_r k_lo_r v_p v_r
        ks_p ks_act ks_dve qs_p qm_act qm_dve xnb_r
        sc_p mx_r mneg_r diag_r st_p exp_r pv_p sums_r att_r wo_p r1_r xh1_r xh1T_p xaT_s xa_hi_r xa_lo_r key_p mask_r
        maskT_p maskT_s b2_p hid_p relu_r y_p ym_r acc0_r acc_r xh2_r fin_pool o_r dve2""".split()
        s = {n: sem(n) for n in names}
        x_in = [s[f"x_in{i}"] for i in range(NG)]

        def col(r):
            return vec[:, r:r + 1]

        def tiles(ap):
            return ap.rearrange("p (t c) -> p t c", c=P)

        def chunk_of(k):
            c = (k % STEPS) // 2
            return slice(c * CHUNK, (c + 1) * CHUNK)

        class Chain:

            def __init__(self, eng, sm, base=0):
                self.eng, self.sm, self.base, self.n = eng, sm, base, 0

            def mark(self, ins):
                ins.then_inc(self.sm, 1)
                self.n += 1

            def then(self, ins):
                self.mark(ins)
                self.eng.wait_ge(self.sm, self.base + self.n)

        def wait(eng, name, value):
            if not isinstance(value, int) or value > 0:
                eng.wait_ge(s[name], value)

        def token_stats(dve, ch, src, slot, first=0, between=None):
            for i in range(TPC):
                last = dve.bn_stats(st[:, slot, first + i, :], src(i))
                if i == TPC - 1:
                    ch.mark(last)
                if between:
                    between()

        class Coefficients:

            LINKS = 12

            def __init__(self, dve, ch, slot, n, at=0):
                self.dve, self.ch, self.i = dve, ch, at
                self.before = ch.n
                self.mean_var = [st[:, slot, 0:n, j] for j in (1, 2, 4, 5)]
                self.tmp = [tmp[:, slot // 2, j, 0:n] for j in range(6)]
                self.rstd, self.nmr = co[:, slot, 0, 0:n], co[:, slot, 1, 0:n]

            def next(self, links=1):
                for _ in range(links):
                    ins = self.link(self.i)
                    self.i += 1
                    if self.i == self.LINKS:
                        return ins
                    self.ch.mark(ins)
                    self.before = self.ch.n

            def finish(self):
                return self.next(self.LINKS - self.i)

            def link(self, i):
                dve = self.dve
                even_m, even_v, odd_m, odd_v = self.mean_var
                msum, mdif, m2, v, y, w = self.tmp
                dve.wait_ge(self.ch.sm, self.ch.base + self.before)
                if i == 0:
                    dve.tensor_tensor(msum, even_m, odd_m, ALU.add)
                    dve.tensor_tensor(mdif, even_m, odd_m, ALU.subtract)
                    return dve.scalar_tensor_tensor(out=m2, in0=even_v, scalar=P * EPS, in1=odd_v,
                                                    op0=ALU.add, op1=ALU.add)
                if i == 1:
                    return dve.scalar_tensor_tensor(out=w, in0=mdif, scalar=0.25, in1=mdif,
                                                    op0=ALU.mult, op1=ALU.mult)
                if i == 2:
                    return dve.scalar_tensor_tensor(out=v, in0=m2, scalar=1.0 / P, in1=w,
                                                    op0=ALU.mult, op1=ALU.add)
                if i == 3:
                    return dve.tensor_scalar(w.bitcast(U32), v.bitcast(U32), 1, None, ALU.logical_shift_right)
                if i == 4:
                    return dve.tensor_scalar(y.bitcast(I32), w.bitcast(I32), -1.0, RSQRT_MAGIC,
                                             ALU.mult, ALU.add)
                if i < 11:
                    step, j = divmod(i - 5, 3)
                    half, one_and_half = RSQRT_STEPS[step]
                    if j == 0:
                        return dve.scalar_tensor_tensor(out=w, in0=y, scalar=-half, in1=y,
                                                        op0=ALU.mult, op1=ALU.mult)
                    if j == 1:
                        return dve.tensor_tensor(w, w, v, ALU.mult)
                    return dve.scalar_tensor_tensor(out=self.rstd if step else y, in0=w, scalar=one_and_half,
                                                    in1=y, op0=ALU.add, op1=ALU.mult)
                return dve.scalar_tensor_tensor(out=self.nmr, in0=msum, scalar=-0.5, in1=self.rstd,
                                                op0=ALU.mult, op1=ALU.mult)

        def normalise(dve, dst, src, slot, first=0, between=None):
            for i in range(TPC):
                last = dve.tensor_scalar(dst(i), src(i), co[:, slot, 0, first + i:first + i + 1],
                                         co[:, slot, 1, first + i:first + i + 1], ALU.mult, ALU.add)
                if between and i < TPC - 1:
                    between()
            return last

        def u_bank(k, layer0):
            return bank[(k // 2) % 2 if layer0 else k % 2]

        def rows_bank(k):
            return bank[2 + k % 4]

        def cols_bank(k):
            return bank[6 + k % 2]

        block = stack.enter_context(nc.Block())

        @block.sync
        def _(sp):
            xr = x.rearrange("b s d -> s b d")
            r = 0
            for v in (cond[0:LAYERS, :], ln_gamma, ln_beta, fusion_b, bq, bk, ln1_g, ln1_b,
                      b1.rearrange("e (c d) -> (e c) d", d=P)):
                v2 = v if len(v.shape) == 2 else v.rearrange("(o d) -> o d", o=1)
                if r == 0:
                    sp.dma_start(x_rows[:, 0:TPC, :], xr[:, 0:TPC, :]).then_inc(x_in[0], 16)
                    sp.dma_start(ctx_rows[:, :, :], ctx_w[0:LAYERS].rearrange("l h i -> h l i")).then_inc(s["ctx_in"], 16)
                sp.dma_start(vec_rows[r:r + v2.shape[0], :], v2).then_inc(s["vec_in"], 16)
                r += v2.shape[0]
            for c in range(1, NG):
                sp.dma_start(x_rows[:, TPC * c:TPC * (c + 1), :], xr[:, TPC * c:TPC * (c + 1), :]).then_inc(x_in[c], 16)
            sp.dma_start(fw_rows[:, :, :], fusion_w.rearrange("h (a i) -> h a i", a=2)).then_inc(s["fw_in"], 16)
            for t, w in ((wq_s, wq), (wk_s, wk), (wv_s, wv), (wo_s, wo)):
                sp.dma_start(t[:, :], w).then_inc(s["attw_in"], 16)
            for t, v in ((bv_bc, bv), (bo_bc, bo), (g2_bc, ln2_g), (b2ln_bc, ln2_b), (rb_bc, router_b)):
                sp.dma_start(t[:, :], v.rearrange("(o d) -> o d", o=1).to_broadcast([P, v.shape[0]])).then_inc(s["bc_in"], 16)
            sp.dma_start(rw_s[:, :], router_w).then_inc(s["rw_in"], 16)
            sp.wait_ge(s["pool_init"], 1)
            for t in range(TPC):
                sp.dma_start(b2_blk[NE * t:NE * t + NE, t, :], b2).then_inc(s["b2_in"], 16)
            sp.dma_start(w1_in, w1.rearrange("e d f -> d e f")).then_inc(s["w1_in"], 16)
            for e in range(NE):
                sp.dma_start(w2_s[:, e, :, :], w2[e].rearrange("(c f) d -> f c d", f=P)).then_inc(s["w2_in"], 16)
            out_v = out.rearrange("b s d -> s b d")
            with sp.Fori(0, NG) as g:
                sp.wait_ge(s["o_r"], g + 1)
                sp.dma_start(out_v[:, bass.ds(g * TPC, TPC), :], o_s[:, :, :]).then_inc(s["out_done"], 16)
            sp.wait_ge(s["out_done"], 16 * NG)

        @block.gpsimd
        def _(pool):
            pool.memset(ident[:, :], 0.0).then_inc(s["ident_done"], 1)
            pool.memset(ident_bf[:, :], 0.0).then_inc(s["ident_done"], 1)
            pool.wait_ge(s["ident_done"], 2)
            for m in (ident[:, :], ident_bf[:, :]):
                pool.affine_select(out=m, in_=m, compare_op=ALU.not_equal, fill=1.0, base=0,
                                   pattern=[[-1, P]], channel_multiplier=1).then_inc(s["ident_done"], 1)
            pool.memset(ones_bf[:, :], 1.0).then_inc(s["ones_done"], 1)
            pool.memset(b2_blk[:, :, :], 0.0).then_inc(s["pool_init"], 1)
            for d in range(2):
                pool.memset(h[d][:, :], 0.0).then_inc(s["pool_init"], 1)
            pool.memset(a_buf[0][:, :, :, 0:1], 0.0).then_inc(s["pool_init"], 1)
            pool.memset(a_buf[1][:, :, :, P - 1:P], 0.0).then_inc(s["pool_init"], 1)
            pool.memset(v_z[:, 0, :], 0.0).then_inc(s["pool_init"], 1)

            def decay(l, k, dirs=1):
                n, i = l * STEPS + k, k % 4
                wait(pool, "gated", n + dirs)
                wait(pool, "s_ready", n - 2)
                pool.tensor_tensor(b_buf[:, i, :], z_buf[:, i, :], t_buf[:, i, :],
                                   ALU.mult).then_inc(s["decay"], dirs)
                for d in ((k % 2,) if dirs == 1 else (0, 1)):
                    keep = slice(1, P) if d == 0 else slice(0, P - 1)
                    pool.tensor_scalar(a_buf[d][:, (k // 2) % 2, :, keep], tiles(z_buf[:, i, :])[:, :, keep],
                                       -1.0, 1.0, ALU.mult, ALU.add).then_inc(s["decay"], 1)

            for k in range(0, STEPS, 2):
                decay(0, k, dirs=2)
            with pool.Fori(1, LAYERS) as l:
                for k in range(STEPS):
                    decay(l, k)

            for t in range(1, TPC):
                pool.memset(v_z[:, t, :], 0.0).then_inc(s["pool_init"], 1)
            pool.wait_ge(s["pool_init"], 5 + TPC)
            for t in range(TPC):
                for o in ones_in_v(t):
                    pool.memset(o, 1.0).then_inc(s["pool_init"], 1)
            pool.wait_ge(s["w1_in"], 16)
            for e in range(NE):
                pool.tensor_scalar(w1_hi[:, e, :], w1_in[:, e, :], 1.0, 1.0, ALU.mult, ALU.mult).then_inc(s["w1_split"], 1)
            for e in range(NE):
                pool.wait_ge(s["w1_split"], NE + e)
                pool.tensor_tensor(w1_lo[:, e, :], w1_in[:, e, :], w1_hi[:, e, :].bitcast(F32),
                                   ALU.subtract).then_inc(s["w1_split"], 1)
            pool.wait_ge(s["bc_in"], 16 * 5)

            def residual(g):
                pool.wait_ge(s["xn_r"], g + 1)
                wait(pool, "r1_r", g)
                pool.tensor_tensor(xnb[:, :, :], xn[:, :, :], bo_bc[:, :].unsqueeze(1).to_broadcast([P, TPC, P]),
                                   ALU.add).then_inc(s["xnb_r"], 1)

            def add_expert(g, e):
                pool.wait_ge(s["ym_r"], NE * g + e + 1)
                if e == 1:
                    pool.wait_ge(s["acc0_r"], g + 1)
                else:
                    pool.wait_ge(s["acc_r"], (NE - 1) * g + e - 1)
                pool.tensor_tensor(acc[:, :, :], acc[:, :, :], ym[:, e % 2, :, :],
                                   ALU.add).then_inc(s["acc_r"], 1)

            def finish(g, last=False):
                pool.wait_ge(s["x1_r"], g + 1)
                pool.tensor_tensor(x1b[:, :, :], x_rows[:, bass.ds(g * TPC, TPC), :],
                                   b2ln_bc[:, :].unsqueeze(1).to_broadcast([P, TPC, P]),
                                   ALU.add).then_inc(s["fin_pool"], 1)
                if last:
                    return
                pool.wait_ge(s["xh2_r"], g + 1)
                wait(pool, "out_done", 16 * g)
                pool.tensor_tensor(o_s[:, :, :], xh2[:, :, :], g2_bc[:, :].unsqueeze(1).to_broadcast([P, TPC, P]),
                                   ALU.mult).then_inc(s["fin_pool"], 1)
                pool.wait_ge(s["fin_pool"], 2 * g + 2)
                pool.tensor_tensor(o_s[:, :, :], o_s[:, :, :], x1b[:, :, :], ALU.add).then_inc(s["o_r"], 1)

            def spread_shift(g, t):
                for j in range(4):
                    pool.wait_ge(s["mneg_r"], NHEAD * g + 4 * t + j + 1)
                    wait(pool, "st_p", NHEAD * g + 4 * t + j - 3)
                    pool.tensor_tensor(diag_of(j), ident_bf[:, :].unsqueeze(1).to_broadcast([P, 4, P]),
                                       mneg[:, t % 2, 4 * j:4 * j + 4].unsqueeze(2).to_broadcast([P, 4, P]),
                                       ALU.mult).then_inc(s["diag_r"], 1)

            def group(g, moe=True, more=True):
                spread_shift(g, 1)
                residual(g)
                spread_shift(g, 2)
                if moe:
                    add_expert(g - 1, 1)
                spread_shift(g, 3)
                if moe:
                    add_expert(g - 1, 2)
                    add_expert(g - 1, 3)
                if more:
                    spread_shift(g + 1, 0)
                if moe:
                    finish(g - 1)

            spread_shift(0, 0)
            group(0, moe=False)
            with pool.Fori(1, NG - 1) as g:
                group(g)
            group(NG - 1, more=False)
            for e in range(1, NE - 1):
                add_expert(NG - 1, e)
            finish(NG - 1, last=True)

        @block.tensor
        def _(pe):
            def turn(dst, src, n=P):
                return pe.transpose(dst, src, ident[0:n, 0:n])

            pe.wait_ge(s["ident_done"], 4)
            pe.wait_ge(s["ctx_in"], 16)
            for l in range(LAYERS):
                last = turn(bank[0][:, l * P:(l + 1) * P], ctx_rows[:, l, :])
            last.then_inc(s["prep_T"], 1)
            pe.wait_ge(s["vec_in"], 16 * 9)
            turn(bank[1][:, 0:NVEC], vec_rows[:, :], NVEC).then_inc(s["prep_T"], 1)

            def turn_x(c):
                pe.wait_ge(s["x_norm"], c + 1)
                for t in range(TPC):
                    last = turn(rows_bank(c)[:, t * P:(t + 1) * P], n_buf[:, c, t, :])
                last.then_inc(s["x_rowsT"], 1)

            def gate_in(l, k, layer0=False):
                n = l * STEPS + k
                if layer0:
                    wait(pe, "gated", n - 2)
                    pe.wait_ge(s["x_cols"], k // 2 + 1)
                    pe.matmul(u_bank(k, True)[:, :], gate_wT[:, 0, 0:P], xT[:, chunk_of(k)],
                              start=True, stop=True).then_inc(s["u_ready"], 2)
                    return
                if k == 0:
                    pe.wait_ge(s["w_cur"], l)
                wait(pe, "gated", n - 1)
                wait(pe, "h_ready", n - STEPS + 1)
                pe.matmul(u_bank(k, False)[:, :], gate_cur[:, 0:P], h[k % 2][:, chunk_of(k)],
                          start=True, stop=True).then_inc(s["u_ready"], 1)

            def to_rows(l, k):
                n, m = l * STEPS + k, l * (STEPS // 2) + k // 2
                if isinstance(l, int) and l == 0 and k < 4:
                    pe.wait_ge(s["x_cols"], k + 1)
                wait(pe, "s_ready", n + 1)
                wait(pe, "n_dve" if k % 2 == 0 else "n_act", m - 1)
                src = h[k % 2][:, chunk_of(k)]
                for t in range(TPC):
                    dst = rows_bank(k)[:, t * P:(t + 1) * P]
                    pe.matmul(dst, s_buf[:, k % 4, t * P:(t + 1) * P], ident[:, :], is_transpose=True,
                              start=True, stop=False)
                    last = pe.matmul(dst, src[:, t * P:(t + 1) * P], ident[:, :], is_transpose=True,
                                     start=False, stop=True)
                last.then_inc(s["rows_ready"], 1)

            def to_cols(l, k):
                n, m = l * STEPS + k, l * (STEPS // 2) + k // 2
                wait(pe, "n_dve" if k % 2 == 0 else "n_act", m + 1)
                wait(pe, "h_ready", n - 1)
                for t in range(TPC):
                    last = turn(cols_bank(k)[:, t * P:(t + 1) * P], n_buf[:, k % 4, t, :])
                last.then_inc(s["cols_ready"], 1)

            turn_x(0)
            pe.wait_ge(s["prep_cols"], 2)
            pe.wait_ge(s["pool_init"], 3)
            def window(l, j, first=0, last=PAIRS, gates=True, layer0=False):
                if first <= j - 2 < last:
                    to_rows(l, 2 * j - 3)
                if gates:
                    gate_in(l, 2 * j, layer0)
                    if not layer0:
                        gate_in(l, 2 * j + 1)
                if first <= j - 3 < last:
                    to_cols(l, 2 * j - 6)
                    to_cols(l, 2 * j - 5)
                if first <= j - 1 < last:
                    to_rows(l, 2 * j - 2)

            for j in range(PAIRS):
                window(0, j, layer0=True)
                for c in ((1, 2), (), (3,), ())[j]:
                    turn_x(c)
                if j == 1:
                    pe.wait_ge(s["fw_in"], 16)
                    for a in range(2):
                        last = turn(bank[6][:, a * P:(a + 1) * P], fw_rows[:, a, :])
                    last.then_inc(s["prep_T"], 1)
                    pe.wait_ge(s["prep_cols"], 3)
            with pe.Fori(1, LAYERS) as l:
                for j in range(PAIRS):
                    window(l, j, first=-PAIRS)

            def fusion(g, dst=bank[6]):
                pe.matmul(dst[:, :], fwT[:, 0, :], h[0][:, bass.ds(g * CHUNK, CHUNK)], start=True, stop=False)
                pe.matmul(dst[:, :], fwT[:, 1, :], h[1][:, bass.ds(g * CHUNK, CHUNK)], start=False,
                          stop=True).then_inc(s["fus_p"], 1)

            def turn_fusion(g, dst=bank[7]):
                pe.wait_ge(s["fus_s"], g + 1)
                for t in range(TPC):
                    last = turn(dst[:, t * P:(t + 1) * P], fus[:, t * P:(t + 1) * P])
                last.then_inc(s["fusT_p"], 1)

            def turn_xn(g, dst=bank[6]):
                pe.wait_ge(s["xn_r"], g + 1)
                for t in range(TPC):
                    last = turn(dst[:, t * P:(t + 1) * P], xn[:, t, :])
                last.then_inc(s["xnT_p"], 1)

            def queries_keys(g, q_bank=bank[6], k_bank=bank[7]):
                pe.wait_ge(s["xnT_s"], g + 1)
                pe.wait_ge(s["x1_r"], g + 1)
                pe.matmul(k_bank[:, :], wk_s[:, :], xnT[:, :], start=True, stop=True).then_inc(s["k_p"], 1)
                pe.matmul(q_bank[:, :], wq_s[:, :], xnT[:, :], start=True, stop=True).then_inc(s["q_p"], 1)

            def stack_keys(g):
                pe.wait_ge(s["k_lo_r"], g + 1)
                if isinstance(g, int) and g == 0:
                    pe.wait_ge(s["q_lo_r"], 1)
                wait(pe, "mx_r", NHEAD * g)
                wait(pe, "exp_r", NHEAD * g)
                for j in range(4):
                    for at, src in ((2, k_hi), (0, k_lo)):
                        w = sel_k[:, j, at:at + 4, :].rearrange("p b c -> p (b c)")
                        last = pe.matmul(bank[j][:, :], w, src[:, :], start=(at > 0), stop=(at == 0))
                    last.then_inc(s["ks_p"], 1)

            def stack_queries(g):
                pe.wait_ge(s["q_lo_r"], g + 1)
                pe.wait_ge(s["ks_act"], 2 * g + 2)
                pe.wait_ge(s["ks_dve"], 2 * g + 2)
                for j in range(4):
                    for at, src in ((1, q_hi), (0, q_lo)):
                        w = sel_q[:, j, at:at + 4, :].rearrange("p b c -> p (b c)")
                        last = pe.matmul(bank[j][:, :], w, src[:, :], start=(at > 0), stop=(at == 0))
                    last.then_inc(s["qs_p"], 1)

            def values(g, dst=bank[7]):
                pe.wait_ge(s["k_lo_r"], g + 1)
                for t in range(TPC):
                    last = pe.matmul(dst[:, t * P:(t + 1) * P], xnT[:, t * P:(t + 1) * P], wv_s[:, :],
                                     start=True, stop=True)
                last.then_inc(s["v_p"], 1)

            def quad_ready(g, j):
                if isinstance(g, int) and g == 0:
                    return ("qm_act", "qm_dve")[j % 2], 1 + j // 2
                return (("qm_act", 3 * g), ("qm_dve", g + 2), ("qm_act", 3 * g + 1), ("qm_act", 3 * g + 2))[j]

            def score_for_max(g, t, j):
                if t == 0:
                    name, value = quad_ready(g, j)
                    pe.wait_ge(s[name], value)
                wait(pe, "mx_r", NHEAD * g + 4 * t + j - 1)
                for i in range(4):
                    last = pe.matmul(bank[j % 2][:, i * P:(i + 1) * P], q_m[:, 4 * j + i, t * P:(t + 1) * P],
                                     k_st[:, j, t * P:(t + 1) * P], start=True, stop=True)
                last.then_inc(s["sc_p"], 1)

            def shifted_scores(g, t):
                for j in range(4):
                    wait(pe, "exp_r", NHEAD * g + 4 * t + j - 1)
                    dst = bank[2 + j % 2]
                    k_t, q_t = k_st[:, j, t * P:(t + 1) * P], q_m[:, 4 * j:4 * j + 4, t * P:(t + 1) * P]
                    pe.matmul(dst[:, :], k_t, q_t, start=True, stop=False, skip_group_check=True)
                    pe.wait_ge(s["diag_r"], NHEAD * g + 4 * t + j + 1)
                    last = pe.matmul(dst[:, :], ones_bf[:, :], diag_of(j), start=False, stop=True, skip_group_check=True)
                    last.then_inc(s["st_p"], 1)
                    if t < TPC - 1:
                        score_for_max(g, t + 1, j)

            def weighted_values(g, t, moe):
                pe.wait_ge(s["exp_r"], NHEAD * g + 4 * t + 4)
                if t == 0:
                    pe.wait_ge(s["v_r"], g + 1)
                    if moe:
                        pe.wait_ge(s["acc0_r"], g)
                else:
                    pe.wait_ge(s["att_r"], TPC * g + t)
                for half in range(2):
                    for i in range(8):
                        hh = 8 * half + i
                        last = pe.matmul(bank[4][:, half * P:(half + 1) * P], v_z[:, t, hh * P:(hh + 1) * P],
                                         probs[:, t % 2, hh, :], start=(i == 0), stop=(i == 7))
                last.then_inc(s["pv_p"], 1)

            def project(g):
                pe.wait_ge(s["att_r"], TPC * (g + 1))
                for t in range(TPC):
                    last = pe.matmul(bank[4][:, t * P:(t + 1) * P], att[:, t * P:(t + 1) * P], wo_s[:, :],
                                     start=True, stop=True)
                last.then_inc(s["wo_p"], 1)

            def back_to_cols(g, moe):
                pe.wait_ge(s["xh1_r"], g + 1)
                if moe:
                    pe.wait_ge(s["relu_r"], NE * FC * g)
                for t in range(TPC):
                    last = turn(bank[6][:, t * P:(t + 1) * P], xh[:, t, :])
                last.then_inc(s["xh1T_p"], 1)

            def router(g):
                pe.wait_ge(s["xaT_s"], g + 1)
                for t in range(TPC):
                    pe.matmul(bank[4][:, t * P:(t + 1) * P], xaT[:, t * P:(t + 1) * P], ident[:, :],
                              start=(t == 0), stop=False, skip_group_check=True)
                wait(pe, "ym_r", NE * g)
                for t in range(TPC):
                    last = pe.matmul(bank[5][:, t:t + 1], xaT[:, t * P:(t + 1) * P], rw_s[:, :],
                                     start=True, stop=True)
                last.then_inc(s["key_p"], 1)

            def turn_mask(g):
                pe.wait_ge(s["mask_r"], g + 1)
                turn(bank[5][0:TPC * NE, 0:P], mask[:, :, :].rearrange("p t e -> p (t e)")).then_inc(s["maskT_p"], 1)

            def routed_bias(g):
                pe.wait_ge(s["maskT_s"], g + 1)
                pe.matmul(bank[4][:, :], maskT[:, :], b2_blk[:, :, :],
                          start=False, stop=True, skip_group_check=True).then_inc(s["b2_p"], 1)

            def hidden(g, e, behind=(), flip=0, pieces=range(FC)):
                for c in pieces:
                    if c < 2 and behind:
                        name, value = behind[c]
                        pe.wait_ge(s[name], value)
                    wait(pe, "relu_r", NE * FC * g + FC * e + c - 1)
                    at, dst = slice(c * P, (c + 1) * P), bank[6 + (c + flip) % 2]
                    pe.matmul(dst[:, :], w1_hi[:, e, at], xa_hi[:, :], start=True, stop=False)
                    pe.matmul(dst[:, :], w1_lo[:, e, at], xa_hi[:, :], start=False, stop=False)
                    if e == 0 and c == 0:
                        pe.wait_ge(s["xa_lo_r"], g + 1)
                    pe.matmul(dst[:, :], w1_hi[:, e, at], xa_lo[:, :], start=False, stop=True).then_inc(s["hid_p"], 1)

            def expert_out(g, e, t):
                if t == 0:
                    pe.wait_ge(s["relu_r"], NE * FC * g + FC * (e + 1))
                    if e:
                        pe.wait_ge(s["ym_r"], NE * g + e)
                for c in range(FC):
                    last = pe.matmul(bank[5][:, t * P:(t + 1) * P], hid[:, e % 2, c, t * P:(t + 1) * P],
                                     w2_s[:, e, c, :], start=(c == 0), stop=(c == FC - 1))
                if t == TPC - 1:
                    last.then_inc(s["y_p"], 1)

            def expert(g, e):
                for t in range(TPC):
                    expert_out(g, e, t)

            def group(g, moe=True, more=True):
                m = g - 1
                shifted_scores(g, 0)
                if more:
                    fusion(g + 1)
                if moe:
                    hidden(m, 1, (("v_r", g + 1), ("fus_s", g + 2)) if more else (), flip=more)
                shifted_scores(g, 1)
                weighted_values(g, 0, moe)
                if more:
                    if moe:
                        pe.wait_ge(s["relu_r"], NE * FC * m + 2 * FC)
                    turn_fusion(g + 1)
                if moe:
                    expert(m, 1)
                shifted_scores(g, 2)
                weighted_values(g, 1, moe)
                if more:
                    turn_xn(g + 1)
                if moe:
                    hidden(m, 2, (("x1_r", g + 2), ("xnT_s", g + 2)) if more else (), flip=more)
                shifted_scores(g, 3)
                if more:
                    if moe:
                        pe.wait_ge(s["relu_r"], NE * FC * m + 3 * FC)
                    queries_keys(g + 1)
                weighted_values(g, 2, moe)
                if more:
                    stack_keys(g + 1)
                else:
                    hidden(m, 3)
                weighted_values(g, 3, moe)
                if more:
                    stack_queries(g + 1)
                if more and moe:
                    hidden(m, 3, (("q_lo_r", g + 2), ("k_lo_r", g + 2)), pieces=range(2))
                if not more:
                    expert_out(m, 2, 0)
                    expert_out(m, 2, 1)
                project(g)
                if more and moe:
                    hidden(m, 3, pieces=range(2, FC))
                if not more:
                    expert_out(m, 2, 2)
                    expert_out(m, 2, 3)
                    expert(m, 3)
                elif moe:
                    expert(m, 2)
                    pe.wait_ge(s["relu_r"], NE * FC * g)
                if more:
                    values(g + 1)
                back_to_cols(g, moe)
                if moe and more:
                    expert(m, 3)
                router(g)
                hidden(g, 0, (("xa_hi_r", g + 1), ("v_r", g + 2)) if more else (("xa_hi_r", g + 1), ("xa_hi_r", g + 1)),
                       pieces=range(3))
                if more:
                    score_for_max(g + 1, 0, 0)
                turn_mask(g)
                hidden(g, 0, pieces=(3,))
                if more:
                    score_for_max(g + 1, 0, 1)
                routed_bias(g)
                if not more:
                    hidden(g, 1)
                expert_out(g, 0, 0)
                if more:
                    score_for_max(g + 1, 0, 2)
                expert_out(g, 0, 1)
                if more:
                    score_for_max(g + 1, 0, 3)
                expert_out(g, 0, 2)
                expert_out(g, 0, 3)

            to_rows(LAYERS - 1, STEPS - 3)
            pe.wait_ge(s["h_ready"], (LAYERS - 1) * STEPS + 2)
            pe.wait_ge(s["gated"], LAYERS * STEPS)
            fusion(0, bank[0])
            to_cols(LAYERS - 1, STEPS - 6)
            to_cols(LAYERS - 1, STEPS - 5)
            to_rows(LAYERS - 1, STEPS - 2)
            turn_fusion(0, bank[1])
            to_rows(LAYERS - 1, STEPS - 1)
            to_cols(LAYERS - 1, STEPS - 4)
            to_cols(LAYERS - 1, STEPS - 3)
            turn_xn(0, bank[0])
            pe.wait_ge(s["attw_in"], 64)
            queries_keys(0, bank[0], bank[1])
            window(LAYERS - 1, PAIRS + 2, gates=False)
            pe.wait_ge(s["ones_done"], 1)
            pe.wait_ge(s["mask_done"], 3)
            stack_keys(0)
            stack_queries(0)
            for j in range(4):
                score_for_max(0, 0, j)
            pe.wait_ge(s["h_ready"], LAYERS * STEPS)
            values(0)
            for name, v in (("w1_split", 2 * NE), ("w2_in", 64), ("b2_in", 64), ("rw_in", 16), ("pool_init", 5 + 3 * TPC)):
                pe.wait_ge(s[name], v)
            group(0, moe=False)
            with pe.Fori(1, NG - 1) as g:
                group(g)
            group(NG - 1, more=False)
            hidden(NG - 1, 2)
            expert(NG - 1, 1)
            hidden(NG - 1, 3)
            expert(NG - 1, 2)
            expert(NG - 1, 3)

        @block.scalar
        def _(act):
            act.wait_ge(s["ident_done"], 4)
            act.activation(key[:, :], ident[:, 0:TPC], ACT.Sigmoid)
            act.wait_ge(s["prep_T"], 1)
            act.activation(gate_wT[:, :, 0:P], tiles(bank[0][:, :]), ACT.Identity).then_inc(s["prep_cols"], 1)
            act.wait_ge(s["prep_T"], 2)
            act.activation(vec[:, :], bank[1][:, 0:NVEC], ACT.Identity)
            act.activation(gate_wT[:, :, P], bank[1][:, R_COND:R_COND + LAYERS], ACT.Identity).then_inc(s["prep_cols"], 1)
            act.wait_ge(s["prep_cols"], 2)

            def x_cols(c):
                act.wait_ge(s["x_rowsT"], c + 1)
                act.activation(xT[:, c * CHUNK:(c + 1) * CHUNK], rows_bank(c)[:, :], ACT.Identity).then_inc(s["x_cols"], 1)

            def gates(l, k, layer0=False):
                n, i = l * STEPS + k, k % 4
                dirs = 2 if layer0 else 1
                wait(act, "u_ready", n + dirs)
                wait(act, "decay", 2 * (n - 2))
                src = u_bank(k, layer0)[:, :]
                bias = gate_wT[:, 0, P:P + 1] if layer0 else gate_cur[:, P:P + 1]
                act.activation(z_buf[:, i, :], src, ACT.Sigmoid, bias=bias)
                act.activation(t_buf[:, i, :], src, ACT.Tanh, bias=bias).then_inc(s["gated"], dirs)

            def norm(l, k):
                n, m = l * STEPS + k, l * (STEPS // 2) + k // 2
                slot = (k // 2) % 2
                wait(act, "coef", m + 1)
                wait(act, "cols_ready", n - 3)
                for t in range(TPC):
                    last = act.activation(n_buf[:, k % 4, t, :], rows_bank(k)[:, t * P:(t + 1) * P], ACT.Identity,
                                          scale=co[:, slot, 0, TPC + t:TPC + t + 1],
                                          bias=co[:, slot, 1, TPC + t:TPC + t + 1])
                last.then_inc(s["n_act"], 1)

            def affine(l, k):
                wait(act, "cols_ready", l * STEPS + k + 1)
                act.activation(h[k % 2][:, chunk_of(k)], cols_bank(k)[:, :], ACT.Identity,
                               scale=col(R_GAMMA), bias=col(R_BETA)).then_inc(s["h_ready"], 1)

            def window(l, j, first=0, last=PAIRS, gated=True, layer0=False):
                if gated:
                    gates(l, 2 * j, layer0)
                if first <= j - 3 < last:
                    norm(l, 2 * j - 5)
                if gated and not layer0:
                    gates(l, 2 * j + 1)
                if first <= j - 3 < last:
                    affine(l, 2 * j - 6)
                    affine(l, 2 * j - 5)

            x_cols(0)
            for j in range(PAIRS):
                window(0, j, layer0=True)
                for c in ((1, 2), (), (3,), ())[j]:
                    x_cols(c)
                if j == 1:
                    act.wait_ge(s["prep_T"], 3)
                    act.activation(fwT[:, :, :], bank[6][:, 0:2 * P].rearrange("p (a h) -> p a h", a=2),
                                   ACT.Identity).then_inc(s["prep_cols"], 1)
            with act.Fori(1, LAYERS) as l:
                act.wait_ge(s["u_ready"], l * STEPS)
                act.wait_ge(s["gated"], l * STEPS)
                act.activation(gate_cur[:, :], gate_wT[:, bass.ds(l, 1), :].rearrange("p o c -> p (o c)"),
                               ACT.Identity).then_inc(s["w_cur"], 1)
                act.wait_ge(s["w_cur"], l)
                for j in range(PAIRS):
                    window(l, j, first=-PAIRS)

            def fusion(g, src=bank[6]):
                act.wait_ge(s["fus_p"], g + 1)
                act.activation(fus[:, :], src[:, :], ACT.Identity, bias=col(R_FB)).then_inc(s["fus_s"], 1)

            def xn_cols(g, src=bank[6]):
                act.wait_ge(s["xnT_p"], g + 1)
                act.activation(xnT[:, :], src[:, :], ACT.Identity).then_inc(s["xnT_s"], 1)

            def queries_keys(g, q_bank=bank[6], k_bank=bank[7]):
                act.wait_ge(s["k_p"], g + 1)
                act.activation(k_hi[:, :], k_bank[:, :], ACT.Identity, bias=col(R_BK)).then_inc(s["k_hi_r"], 1)
                act.wait_ge(s["q_p"], g + 1)
                act.activation(q_hi[:, :], q_bank[:, :], ACT.Identity, bias=col(R_BQ)).then_inc(s["q_hi_r"], 1)

            def key_stacks(g):
                for j in (0, 2):
                    act.wait_ge(s["ks_p"], 4 * g + j + 1)
                    act.activation(k_st[:, j, :], bank[j][:, :], ACT.Identity).then_inc(s["ks_act"], 1)

            def query_heads(g, n):
                j = QUADS_ACT[not isinstance(g, int) or g > 0][n]
                act.wait_ge(s["qs_p"], 4 * g + j + 1)
                for i in range(4):
                    last = act.activation(q_m[:, 4 * j + i, :], bank[j][:, :], ACT.Identity, scale=quad_mask[:, i:i + 1])
                last.then_inc(s["qm_act"], 1)

            def exps(g, t):
                wait(act, "pv_p", TPC * g + t - 1)
                for j in range(4):
                    act.wait_ge(s["st_p"], NHEAD * g + 4 * t + j + 1)
                    act.activation(probs[:, t % 2, 4 * j:4 * j + 4, :], tiles(bank[2 + j % 2][:, :]), ACT.Exp,
                                   scale=SCALE).then_inc(s["exp_r"], 1)

            def prob_sums(g, t):
                act.wait_ge(s["pv_p"], TPC * g + t + 1)
                act.activation(sums[64:128, :], bank[4][64:128, 0:P], ACT.Identity)
                act.activation(sums[0:64, :], bank[4][0:64, P:2 * P], ACT.Identity).then_inc(s["sums_r"], 1)

            def xa_cols(g):
                act.wait_ge(s["xh1T_p"], g + 1)
                for dst, done in ((xaT, "xaT_s"), (xa_hi, "xa_hi_r")):
                    act.activation(dst[:, :], bank[6][:, :], ACT.Identity, scale=col(R_G1),
                                   bias=col(R_B1LN)).then_inc(s[done], 1)

            def relu(g, e, flip=0, pieces=range(FC)):
                for c in pieces:
                    act.wait_ge(s["hid_p"], NE * FC * g + FC * e + c + 1)
                    act.activation(hid[:, e % 2, c, :], bank[6 + (c + flip) % 2][:, :], ACT.Relu,
                                   bias=col(R_B1 + FC * e + c)).then_inc(s["relu_r"], 1)

            def mask_rows(g):
                act.wait_ge(s["maskT_p"], g + 1)
                act.activation(maskT[:, :], bank[5][0:TPC * NE, 0:P], ACT.Identity).then_inc(s["maskT_s"], 1)

            def group(g, moe=True, more=True):
                m = g - 1
                exps(g, 0)
                if more:
                    fusion(g + 1)
                if moe:
                    relu(m, 1, flip=more)
                exps(g, 1)
                prob_sums(g, 0)
                exps(g, 2)
                prob_sums(g, 1)
                if more:
                    xn_cols(g + 1)
                if moe:
                    relu(m, 2, flip=more)
                exps(g, 3)
                if more:
                    queries_keys(g + 1)
                prob_sums(g, 2)
                if more:
                    key_stacks(g + 1)
                else:
                    relu(m, 3)
                prob_sums(g, 3)
                if more:
                    query_heads(g + 1, 0)
                    if moe:
                        relu(m, 3, pieces=range(2))
                    query_heads(g + 1, 1)
                    if moe:
                        relu(m, 3, pieces=range(2, FC))
                    query_heads(g + 1, 2)
                xa_cols(g)
                relu(g, 0, pieces=range(3))
                mask_rows(g)
                relu(g, 0, pieces=(3,))

            norm(LAYERS - 1, STEPS - 5)
            fusion(0, bank[0])
            affine(LAYERS - 1, STEPS - 6)
            affine(LAYERS - 1, STEPS - 5)
            window(LAYERS - 1, PAIRS + 1, gated=False)
            norm(LAYERS - 1, STEPS - 1)
            xn_cols(0, bank[0])
            queries_keys(0, bank[0], bank[1])
            affine(LAYERS - 1, STEPS - 2)
            affine(LAYERS - 1, STEPS - 1)
            key_stacks(0)
            act.wait_ge(s["mask_done"], 3)
            act.wait_ge(s["s_ready"], LAYERS * STEPS)
            act.wait_ge(s["cols_ready"], LAYERS * STEPS)
            query_heads(0, 0)
            query_heads(0, 1)
            group(0, moe=False)
            with act.Fori(1, NG - 1) as g:
                group(g)
            group(NG - 1, more=False)
            for e in range(1, NE):
                relu(NG - 1, e)

        @block.vector
        def _(dve):
            ch = Chain(dve, s["dve1"])
            def no_link():
                pass

            def x_stats(chunks):
                for i, c in enumerate(chunks):
                    dve.wait_ge(x_in[c], 16)
                    token_stats(dve, ch, lambda t: x_rows[:, TPC * c + t, :], 2, TPC * i)
                return Coefficients(dve, ch, 2, TPC * len(chunks))

            def x_norm(chunks, links):
                ch.then(links.finish())
                for i, c in enumerate(chunks):
                    normalise(dve, lambda t: n_buf[:, c, t, :], lambda t: x_rows[:, TPC * c + t, :],
                              2, TPC * i).then_inc(s["x_norm"], 1)

            for chunks in ((0,), (1, 2)):
                x_norm(chunks, x_stats(chunks))
            dve.wait_ge(s["ident_done"], 4)
            dve.reduce_sum(head_mask[:, :], ident[:, :].rearrange("p (h y) -> p h y", y=HD),
                           AX.X).then_inc(s["mask_done"], 1)
            dve.wait_ge(s["mask_done"], 1)
            dve.reduce_sum(quad_mask[:, :], head_mask[:, :].rearrange("p (q i) -> p i q", i=4),
                           AX.X).then_inc(s["mask_done"], 1)
            for blocks, n, value in ((sel_k[:, :, 0:2, :], 2, 0.0), (sel_k[:, :, 4:6, :], 2, 0.0), (sel_k[:, :, 2:4, :], 2, 1.0),
                                     (sel_q[:, :, 0::2, :], 3, 0.0), (sel_q[:, :, 1::2, :], 2, 1.0)):
                eye = ident[:, :].rearrange("p (j c) -> p j c", c=32).unsqueeze(2).to_broadcast([P, 4, n, 32])
                last = dve.tensor_scalar(blocks, eye, value, None, ALU.mult)
            last.then_inc(s["mask_done"], 1)
            dve.wait_ge(s["pool_init"], 5)

            def clip(ch, l, k, layer0=False):
                n, d = l * STEPS + k, k % 2
                a = a_buf[d][:, (k // 2) % 2, :, slice(1, P) if d == 0 else slice(0, P - 1)]
                wait(dve, "decay", 2 * (n + (2 if layer0 and d == 0 else 1)))
                ch.mark(dve.tensor_scalar(a, a, CLAMP_LO, CLAMP_HI, ALU.max, ALU.min))
                return ch.n

            def scan(ch, l, k, clipped, layer0=False):
                n, d, i = l * STEPS + k, k % 2, ((k - k % 2) if layer0 else k) % 4
                dve.wait_ge(ch.sm, ch.base + clipped)
                wait(dve, "rows_ready", n - 3)
                a = a_buf[d][:, (k // 2) % 2, :, :].rearrange("p t c -> p (t c)")
                b, out_s = b_buf[:, i, :], s_buf[:, k % 4, :]
                if d:
                    a, b, out_s = a[:, ::-1], b[:, ::-1], out_s[:, ::-1]
                dve.tensor_tensor_scan(out_s, a, b, 0.0, ALU.mult, ALU.add).then_inc(s["s_ready"], 1)

            def stats(ch, l, k, between):
                wait(dve, "rows_ready", l * STEPS + k + 1)
                token_stats(dve, ch, lambda i: rows_bank(k)[:, i * P:(i + 1) * P], (k // 2) % 2, TPC * (k % 2),
                            between)

            def norm(l, k, between):
                wait(dve, "coef", l * PAIRS + k // 2 + 1)
                if isinstance(l, int) and l == 0:
                    dve.wait_ge(s["x_rowsT"], NG)
                wait(dve, "cols_ready", l * STEPS + k - 3)
                normalise(dve, lambda i: n_buf[:, k % 4, i, :], lambda i: rows_bank(k)[:, i * P:(i + 1) * P],
                          (k // 2) % 2, between=between).then_inc(s["n_dve"], 1)

            SPLIT = 7

            def window(ch, l, j, first=0, last=PAIRS, scans=True, layer0=False, side=None,
                       before_norm=no_link):
                old = new = None
                if first <= j - 2 < last:
                    wait(dve, "n_act", l * PAIRS + j - 3)
                    old = Coefficients(dve, ch, j % 2, 2 * TPC, at=SPLIT)

                def old_link():
                    if old and old.i < old.LINKS:
                        final = old.next()
                        if final:
                            final.then_inc(s["coef"], 1)

                def new_link():
                    if new and new.i < SPLIT:
                        new.next()

                if first <= j - 1 < last:
                    for k in (2 * j - 2, 2 * j - 1):
                        stats(ch, l, k, between=old_link)
                    new = Coefficients(dve, ch, (j - 1) % 2, 2 * TPC)
                while old and old.i < old.LINKS:
                    old_link()
                    if side:
                        side.link()
                before_norm()
                if old:
                    norm(l, 2 * j - 4, between=new_link)
                if scans:
                    for k in (2 * j, 2 * j + 1):
                        clipped = clip(ch, l, k, layer0)
                        new_link()
                        if side:
                            side.next(2)
                        scan(ch, l, k, clipped, layer0)
                        new_link()
                        if side:
                            side.next(2)
                while new and new.i < SPLIT:
                    new_link()

            for j in range(PAIRS):
                links = x_stats((3,)) if j == 0 else None
                window(ch, 0, j, layer0=True, side=links)
                if j == 0:
                    x_norm((3,), links)
            PER_LAYER = 2 * STEPS + PAIRS * (Coefficients.LINKS - 1)
            before = ch.n
            with dve.Fori(1, LAYERS) as l:
                ch = Chain(dve, s["dve1"], (l - 1) * PER_LAYER + before)
                for j in range(PAIRS):
                    window(ch, l, j, first=-PAIRS)
                assert ch.n == PER_LAYER
            class Norm:

                LINKS = Coefficients.LINKS

                def __init__(self, ch, src):
                    self.src = src
                    token_stats(dve, ch, src, 2)
                    self.co = Coefficients(dve, ch, 2, TPC)

                def link(self, n=1):
                    if self.co.i + n < self.co.LINKS:
                        self.co.next(n)

                def finish(self, ch, dst, name):
                    ch.then(self.co.finish())
                    normalise(dve, dst, self.src, 2).then_inc(s[name], 1)

            def front_rows(ch, g, fused=bank[7]):
                dve.wait_ge(s["fusT_p"], g + 1)
                x_g = x_rows[:, bass.ds(g * TPC, TPC), :]
                ch.then(dve.tensor_tensor(x1[:, :, :], tiles(fused[:, :]), x_g, ALU.add))
                norm = Norm(ch, lambda i: x1[:, i, :])
                dve.tensor_copy(x_g, x1[:, :, :]).then_inc(s["x1_r"], 1)
                return norm

            def finish_front(ch, g, norm):
                wait(dve, "xnb_r", g)
                norm.finish(ch, lambda i: xn[:, i, :], "xn_r")

            ch = Chain(dve, s["dve1"], before + (LAYERS - 1) * PER_LAYER)
            window(ch, LAYERS - 1, PAIRS, scans=False)
            front = front_rows(ch, 0, fused=bank[1])
            window(ch, LAYERS - 1, PAIRS + 1, scans=False, side=front, before_norm=lambda: finish_front(ch, 0, front))

            def low_parts(g, q_bank=bank[6], k_bank=bank[7]):
                for lo, hi, src, bias, ready, done in ((k_lo, k_hi, k_bank, R_BK, "k_hi_r", "k_lo_r"),
                                                       (q_lo, q_hi, q_bank, R_BQ, "q_hi_r", "q_lo_r")):
                    dve.wait_ge(s[ready], g + 1)
                    dve.scalar_tensor_tensor(out=lo[:, :], in0=src[:, :], scalar=col(bias), in1=hi[:, :].bitcast(F32),
                                             op0=ALU.add, op1=ALU.subtract).then_inc(s[done], 1)

            def key_stacks(g):
                for j in (1, 3):
                    dve.wait_ge(s["ks_p"], 4 * g + j + 1)
                    dve.tensor_copy(k_st[:, j, :], bank[j][:, :]).then_inc(s["ks_dve"], 1)

            def query_heads(g):
                for j in QUADS_DVE[not isinstance(g, int) or g > 0]:
                    dve.wait_ge(s["qs_p"], 4 * g + j + 1)
                    for i in range(4):
                        last = dve.tensor_scalar(q_m[:, 4 * j + i, :], bank[j][:, :], quad_mask[:, i:i + 1], None,
                                                 ALU.mult)
                    last.then_inc(s["qm_dve"], 1)

            def value_rows(g, src_bank=bank[7]):
                dve.wait_ge(s["v_p"], g + 1)
                for half, dst in enumerate(v_dims):
                    at = slice(64 * half, 64 * half + 64)
                    src = tiles(src_bank[:, :])[:, :, at].rearrange("p t (h y) -> p t h y", y=HD)
                    bias = bv_bc[:, at].rearrange("p (h y) -> p h y", y=HD).unsqueeze(1).to_broadcast([P, TPC, 8, HD])
                    last = dve.tensor_tensor(dst, src, bias, ALU.add)
                last.then_inc(s["v_r"], 1)

            def maxima(g, t, between=no_link):
                def negate(j):
                    at = slice(4 * j, 4 * j + 4)
                    dve.wait_ge(s["mx_r"], NHEAD * g + 4 * t + j + 1)
                    dve.tensor_scalar(mneg[:, t % 2, at], mx[:, t % 2, at], -1.0, None, ALU.mult).then_inc(s["mneg_r"], 1)

                for j in range(4):
                    dve.wait_ge(s["sc_p"], NHEAD * g + 4 * t + j + 1)
                    dve.reduce_max(mx[:, t % 2, 4 * j:4 * j + 4], tiles(bank[j % 2][:, :]),
                                   AX.X).then_inc(s["mx_r"], 1)
                    between()
                    if j == 0:
                        wait(dve, "diag_r", NHEAD * g + 4 * t - 4)
                    else:
                        negate(j - 1)
                negate(3)

            def attended(ch, g, t, between=no_link):
                dve.wait_ge(s["sums_r"], TPC * g + t + 1)
                if t == 0:
                    wait(dve, "wo_p", g)
                ch.mark(dve.reciprocal(sums[:, :], sums[:, :]))
                between()
                dve.wait_ge(ch.sm, ch.base + ch.n)
                at = slice(t * P, (t + 1) * P)
                dve.tensor_tensor(att[0:64, at], bank[4][0:64, 0:P], sums[64:128, :], ALU.mult)
                dve.tensor_tensor(att[64:128, at], bank[4][64:128, P:2 * P], sums[0:64, :],
                                  ALU.mult).then_inc(s["att_r"], 1)

            def first_norm(ch, g):
                dve.wait_ge(s["wo_p"], g + 1)
                dve.wait_ge(s["xnb_r"], g + 1)
                dve.tensor_tensor(r1[:, :, :], tiles(bank[4][:, :]), xnb[:, :, :], ALU.add).then_inc(s["r1_r"], 1)
                dve.wait_ge(s["r1_r"], g + 1)
                return Norm(ch, lambda i: r1[:, i, :])

            def floor(ch, dst, src, flag):
                ch.then(dve.tensor_copy(ki[:, :], src))
                ch.then(dve.tensor_copy(dst, ki[:, :]))
                ch.then(dve.tensor_tensor(flag, dst, src, ALU.is_gt))
                ch.then(dve.tensor_tensor(dst, dst, flag, ALU.subtract))

            def xa_low(g):
                dve.wait_ge(s["xa_hi_r"], g + 1)
                dve.tensor_tensor(xa_lo[:, :], xaT[:, :], xa_hi[:, :].bitcast(F32), ALU.subtract).then_inc(s["xa_lo_r"], 1)

            def route(ch, g):
                dve.wait_ge(s["key_p"], g + 1)
                ch.then(dve.tensor_scalar(key[:, :], bank[5][:, 0:TPC], rb_bc[:, :], None, ALU.add))
                fl, quarter, fq, flag = (kf[:, i, :] for i in range(4))
                floor(ch, fl, key[:, :], flag)
                ch.then(dve.tensor_scalar(quarter, fl, 1.0 / NE, None, ALU.mult))
                floor(ch, fq, quarter, flag)
                ch.then(dve.scalar_tensor_tensor(out=fl, in0=fq, scalar=-float(NE), in1=fl, op0=ALU.mult, op1=ALU.add))
                wait(dve, "maskT_p", g)
                for e in range(NE):
                    last = dve.tensor_scalar(mask[:, :, e], fl, float(e), None, ALU.is_equal)
                last.then_inc(s["mask_r"], 1)

            def masked(g, e):
                dve.wait_ge(s["y_p"], NE * g + e + 1)
                if e == 3:
                    dve.wait_ge(s["acc_r"], 3 * g + 1)
                dve.tensor_tensor(ym[:, e % 2, :, :], tiles(bank[5][:, :]),
                                  mask[:, :, e:e + 1].to_broadcast([P, TPC, P]), ALU.mult).then_inc(s["ym_r"], 1)

            def first_expert(g):
                masked(g, 0)
                dve.wait_ge(s["b2_p"], g + 1)
                dve.wait_ge(s["ym_r"], NE * g + 1)
                dve.tensor_tensor(acc[:, :, :], ym[:, 0, :, :], tiles(bank[4][:, :]), ALU.add).then_inc(s["acc0_r"], 1)

            def second_norm(ch, g):
                dve.wait_ge(s["acc_r"], 3 * g + 3)
                return Norm(ch, lambda i: acc[:, i, :])

            def finish_second(ch, g, norm):
                wait(dve, "o_r", g)
                dve.wait_ge(s["xh1T_p"], min(g + 2, NG) if isinstance(g, int) else g + 2)
                norm.finish(ch, lambda i: xh2[:, i, :], "xh2_r")

            def group(ch, g, moe=True, more=True):
                m = g - 1
                maxima(g, 1)
                if moe:
                    first_expert(m)
                maxima(g, 2)
                norm = front_rows(ch, g + 1) if more else None
                link = norm.link if more else no_link
                attended(ch, g, 0, between=link)
                link()
                if moe:
                    masked(m, 1)
                    link()
                maxima(g, 3, between=link)
                if more:
                    finish_front(ch, g + 1, norm)
                attended(ch, g, 1)
                if more:
                    low_parts(g + 1)
                attended(ch, g, 2)
                if more:
                    key_stacks(g + 1)
                attended(ch, g, 3)
                if more:
                    query_heads(g + 1)
                norm = first_norm(ch, g)
                if not more:
                    norm.link(1)
                    masked(m, 2)
                wait(dve, "xh1T_p", g)
                norm.finish(ch, lambda i: xh[:, i, :], "xh1_r")
                if moe and more:
                    masked(m, 2)
                if more:
                    value_rows(g + 1)
                if moe:
                    masked(m, 3)
                xa_low(g)
                route(ch, g)
                norm = second_norm(ch, m) if moe else None
                if more:
                    maxima(g + 1, 0, between=norm.link if moe else no_link)
                if moe:
                    finish_second(ch, m, norm)

            ch = Chain(dve, s["dve2"])
            low_parts(0, bank[0], bank[1])
            key_stacks(0)
            dve.wait_ge(s["s_ready"], LAYERS * STEPS)
            dve.wait_ge(s["cols_ready"], LAYERS * STEPS)
            query_heads(0)
            maxima(0, 0)
            dve.wait_ge(s["pool_init"], 5 + 3 * TPC)
            dve.wait_ge(s["bc_in"], 16 * 5)
            value_rows(0)
            group(ch, 0, moe=False)
            before, PER_GROUP = ch.n, 3 * (Norm.LINKS + 1) + 1 + TPC + 11
            with dve.Fori(1, NG - 1) as g:
                ch = Chain(dve, s["dve2"], (g - 1) * PER_GROUP + before)
                group(ch, g)
                assert ch.n == PER_GROUP, ch.n
            ch = Chain(dve, s["dve2"], before + (NG - 2) * PER_GROUP)
            group(ch, NG - 1, more=False)
            first_expert(NG - 1)
            for e in range(1, NE):
                masked(NG - 1, e)
            dve.wait_ge(s["ym_r"], NE * NG)
            dve.wait_ge(s["acc_r"], 3 * NG - 1)
            dve.tensor_tensor(acc[:, :, :], acc[:, :, :], ym[:, (NE - 1) % 2, :, :], ALU.add).then_inc(s["acc_r"], 1)
            finish_second(ch, NG - 1, second_norm(ch, NG - 1))
            dve.wait_ge(s["xh2_r"], NG)
            dve.wait_ge(s["out_done"], 16 * (NG - 1))
            ch.then(dve.tensor_tensor(o_s[:, :, :], xh2[:, :, :], g2_bc[:, :].unsqueeze(1).to_broadcast([P, TPC, P]),
                                      ALU.mult))
            dve.wait_ge(s["fin_pool"], 2 * NG - 1)
            dve.tensor_tensor(o_s[:, :, :], o_s[:, :, :], x1b[:, :, :], ALU.add).then_inc(s["o_r"], 1)


_P = "L0_ffn_"
_INS = ["x", "ctx_1024", "cond_1024", "L0_xcond_fusion_W", "L0_xcond_fusion_b", "L0_xcond_ln_gamma",
        "L0_xcond_ln_beta"] + [_P + n for n in (
            "Wq", "bq", "Wk", "bk", "Wv", "bv", "Wo", "bo", "router_w", "router_b", "W1", "b1", "W2", "b2",
            "ln1_g", "ln1_b", "ln2_g", "ln2_b")]


def kernel(**inputs):
    import numpy as _np
    import concourse.bacc as _bacc
    from concourse import mybir as _mybir
    from concourse.bass_utils import run_bass_kernel_spmd as _run

    nc = _bacc.Bacc("TRN2", target_bir_lowering=False, num_devices=1)
    arrays, args = {}, []
    for name in _INS:
        a = _np.ascontiguousarray(inputs[name])
        arrays[f"in_{name}_dram"] = a
        args.append(nc.dram_tensor(f"in_{name}_dram", a.shape, _mybir.dt.from_np(a.dtype), kind="ExternalInput").ap())
    shape = _np.shape(inputs["x"])
    args.append(nc.dram_tensor("out_dram", shape, _mybir.dt.float32, kind="ExternalOutput").ap())
    build(nc, *args)
    r = _run(nc, [arrays], core_ids=[0])
    return r.results[0]["out_dram"]
```
